# Optimizing a Trainium2 kernel written in Bass

```python
import numpy as np
import jax
import jax.numpy as jnp

def _softmax(x, axis=-1):
    return jax.nn.softmax(x, axis=axis)

def _gelu(x):
    return jax.nn.gelu(x, approximate=True)

def _silu(x):
    return jax.nn.silu(x)

def _sigmoid(x):
    return jax.nn.sigmoid(x)

def _layernorm(x, axis=-1, eps=1e-05):
    m = jnp.mean(x, axis=axis, keepdims=True)
    v = jnp.var(x, axis=axis, keepdims=True)
    return (x - m) / jnp.sqrt(v + eps)

def _scatter_add(tgt, idx, src, axis=0):
    return tgt.at[idx].add(src)

def _segment_sum(src, seg, n):
    return jax.ops.segment_sum(src, seg, n)
kernel_name = 'mk_xattn_ffn_d1_seqx_r8_a82ac8'

def setup_inputs(seed: int=0):
    np.random.seed(seed)
    _w = jnp.asarray

    def _rec_inputs():
        import jax
        import jax.numpy as jnp
        _rk = jax.random.key(seed)
        x = -0.0005207 + 1.001 * jax.random.normal(jax.random.fold_in(_rk, 1), (4, 256, 512), jnp.float32)
        _lenS = 256 - jax.random.randint(jax.random.fold_in(_rk, 7), (4,), 0, max(1, 256 // 4) + 1, jnp.int32)
        _lenS2 = 1601 - jax.random.randint(jax.random.fold_in(_rk, 8), (4,), 0, max(1, 1601 // 4) + 1, jnp.int32)
        _ctx_4096P = jax.random.normal(jax.random.fold_in(_rk, 11), (4, 16, 512), jnp.float32)
        _ctx_4096c = jax.random.dirichlet(jax.random.fold_in(_rk, 511), 0.3 * jnp.ones((16,), jnp.float32), (4, 1601))
        _ctx_4096t = jnp.einsum('bsk,bkd->bsd', _ctx_4096c, _ctx_4096P)
        _ctx_4096t = _ctx_4096t * jax.lax.rsqrt(jnp.mean(jnp.square(_ctx_4096t)) + 1e-12) * 0.953939
        ctx_4096 = -0.00010331 + 0.999899 * (_ctx_4096t + 0.3 * jax.random.normal(jax.random.fold_in(_rk, 611), (4, 1601, 512), jnp.float32))
        return (x, ctx_4096)
    x, ctx_4096 = _rec_inputs()

    def _L0_xattn_setup():
        import jax, jax.numpy as jnp
        import numpy as np
        B, Q, D = (8, 64, 512)
        CTX = 512
        H, KV, HD = (16, 4, 96)
        G = H // KV
        key = jax.random.key(seed)
        ks = jax.random.split(key, 6)
        s = 0.02
        return {'latents': jax.random.normal(ks[0], (B, Q, D), jnp.float32), 'context': jax.random.normal(ks[1], (B, CTX, D), jnp.float32), 'Wq': jax.random.normal(ks[2], (H * HD, D), jnp.float32) * s, 'Wk': jax.random.normal(ks[3], (KV * HD, D), jnp.float32) * s, 'Wv': jax.random.normal(ks[4], (KV * HD, D), jnp.float32) * s, 'Wo': jax.random.normal(ks[5], (D, H * HD), jnp.float32) * s}
    _L0_xattn_all = _L0_xattn_setup()
    _L0_xattn_in = {k: v for k, v in _L0_xattn_all.items() if k in ('Wq', 'Wk', 'Wv', 'Wo')}
    del _L0_xattn_all

    def _L0_ffn_setup():
        import jax, jax.numpy as jnp
        import numpy as np
        TOP_K = 2
        key = jax.random.key(seed)
        k0, k1, k2 = jax.random.split(key, 3)
        B, S, D, H, E = (4, 256, 512, 512, 8)
        sc = 1.0 / np.sqrt(D).astype(np.float32)
        x = jax.random.normal(k0, (B, S, D), dtype=jnp.float32)
        W_gate = jax.random.normal(k1, (D, E), dtype=jnp.float32) * sc
        b_gate = jnp.zeros((E,), dtype=jnp.float32)
        W_e = jax.random.normal(k2, (E, D, H), dtype=jnp.float32) * sc
        b_e = jnp.zeros((E, H), dtype=jnp.float32)
        return {'x': x, 'W_gate': W_gate, 'b_gate': b_gate, 'W_e': W_e, 'b_e': b_e}
    _L0_ffn_all = _L0_ffn_setup()
    _L0_ffn_in = {k: v for k, v in _L0_ffn_all.items() if k in ('W_gate', 'b_gate', 'W_e', 'b_e')}
    del _L0_ffn_all
    return {'x': x, 'ctx_4096': ctx_4096, 'L0_xattn_Wq': _L0_xattn_in['Wq'], 'L0_xattn_Wk': _L0_xattn_in['Wk'], 'L0_xattn_Wv': _L0_xattn_in['Wv'], 'L0_xattn_Wo': _L0_xattn_in['Wo'], 'L0_ffn_W_gate': _L0_ffn_in['W_gate'], 'L0_ffn_b_gate': _L0_ffn_in['b_gate'], 'L0_ffn_W_e': _L0_ffn_in['W_e'], 'L0_ffn_b_e': _L0_ffn_in['b_e']}

def reference(x, ctx_4096, L0_xattn_Wq, L0_xattn_Wk, L0_xattn_Wv, L0_xattn_Wo, L0_ffn_W_gate, L0_ffn_b_gate, L0_ffn_W_e, L0_ffn_b_e):
    import jax
    import jax.numpy as jnp

    def _L0_xattn_ref(latents, context, Wq, Wk, Wv, Wo):
        import jax, jax.numpy as jnp
        import numpy as np
        B, Q, D = (8, 64, 512)
        CTX = 512
        H, KV, HD = (16, 4, 96)
        G = H // KV
        b, q_len, _ = latents.shape
        hidden = jnp.concatenate([context, latents], axis=1)
        s_len = hidden.shape[1]
        q = (latents @ Wq.T).reshape(b, q_len, H, HD)
        k = (hidden @ Wk.T).reshape(b, s_len, KV, HD)
        v = (hidden @ Wv.T).reshape(b, s_len, KV, HD)
        q = q.transpose(0, 2, 1, 3).reshape(b, KV, G, q_len, HD)
        k = k.transpose(0, 2, 1, 3)
        v = v.transpose(0, 2, 1, 3)
        scale = 1.0 / jnp.sqrt(jnp.asarray(HD, q.dtype))
        scores = jnp.einsum('bkgqd,bksd->bkgqs', q, k) * scale
        attn = jax.nn.softmax(scores.astype(jnp.float32), axis=-1).astype(q.dtype)
        out = jnp.einsum('bkgqs,bksd->bkgqd', attn, v)
        out = out.reshape(b, H, q_len, HD).transpose(0, 2, 1, 3).reshape(b, q_len, H * HD)
        return out @ Wo.T

    def _L0_ffn_ref(x, W_gate, b_gate, W_e, b_e):
        import jax, jax.numpy as jnp
        import numpy as np
        TOP_K = 2
        logits = x @ W_gate + b_gate
        _, top_idx = jax.lax.top_k(logits, TOP_K)
        y_all = jax.nn.relu(jnp.einsum('bsd,edh->bseh', x, W_e) + b_e)
        y = jnp.take_along_axis(y_all, top_idx[..., None], axis=2)
        return y.mean(axis=2)
    x = x + _L0_xattn_ref(_layernorm(x, axis=-1), ctx_4096, L0_xattn_Wq, L0_xattn_Wk, L0_xattn_Wv, L0_xattn_Wo)
    x = x + _L0_ffn_ref(_layernorm(x, axis=-1), L0_ffn_W_gate, L0_ffn_b_gate, L0_ffn_W_e, L0_ffn_b_e)
    return x

_drawn_inputs = setup_inputs


def setup_inputs(seed=0):
    import zlib

    import numpy as np

    out = dict(_drawn_inputs(seed))
    spreads = {'L0_ffn_b_gate': (0.0, 0.1), 'L0_ffn_b_e': (0.0, 0.1)}
    factors = {}
    for name, (base, spread) in spreads.items():
        noise = np.random.default_rng([zlib.crc32(name.encode()), seed]).standard_normal(out[name].shape)
        drawn = base * np.exp(spread * noise) if base else spread * noise
        out[name] = jnp.asarray(drawn.astype(out[name].dtype))
    for name, factor in factors.items():
        out[name] = (out[name] * factor).astype(out[name].dtype)
    return out
```

```python
from contextlib import ExitStack

import concourse.bass as bass
from concourse import mybir

F32 = mybir.dt.float32
F32R = mybir.dt.float32r
ALU = mybir.AluOpType
ACT = mybir.ActivationFunctionType
AX_X = mybir.AxisListType.X

P = 128
BANK = 512
EPS = 1e-5


def three_passes(w_hi, w_lo, m_hi, m_lo):
    return ((w_hi, m_hi), (w_hi, m_lo), (w_lo, m_hi))


def split_product(nc, out, blocks):
    pairs = [pair for block in blocks for pair in three_passes(*block)]
    for n, (stationary, moving) in enumerate(pairs):
        last = nc.tensor.matmul(out, stationary, moving, start=(n == 0), stop=(n == len(pairs) - 1))
    return last


def latent_norm_and_queries(nc, x, wq, ident_in, xt_dram, q_dram):
    T, D = x.shape
    QD = wq.shape[1]
    NT, NC, NM = T // P, D // P, QD // P
    HALVES = T // BANK
    x_v = x.rearrange("(t p) d -> p t d", p=P)
    wq_v = wq.rearrange("(c p) m -> p c m", p=P)
    xt_v = xt_dram.rearrange("(c p) t -> p c t", p=P)

    with ExitStack() as ctx:
        def sb(name, shape, dt=F32):
            return ctx.enter_context(nc.sbuf_tensor(name, shape, dt))

        def sem(name):
            return ctx.enter_context(nc.semaphore(name))

        x_sb = sb("n1_x", [P, NT, D])
        ident = sb("n1_ident", [P, P])
        stats = sb("n1_stats", [P, NT, 6])
        mean_var = sb("n1_mean_var", [P, NT, 2])
        var_eps = sb("n1_var_eps", [P, NT])
        std = sb("n1_std", [P, NT])
        rstd = sb("n1_rstd", [P, NT])
        xn = sb("n1_xn", [P, 2, D])
        xt_hi = sb("n1_xt_hi", [P, NC, T], F32R)
        xt_lo = sb("n1_xt_lo", [P, NC, T], F32R)
        xt_raw = sb("n1_xt_raw", [P, 2, NC, P])
        wq_raw = sb("q_w_raw", [P, 2, NC, P])
        wq_hi = sb("q_w_hi", [P, 2, NC, P], F32R)
        wq_lo = sb("q_w_lo", [P, 2, NC, P], F32R)
        q_sb = sb("q_sb", [P, 4, BANK])
        xt_ps = ctx.enter_context(nc.psum_tensor("n1_xt_ps", [P, 2, NC, P], F32))
        q_ps = ctx.enter_context(nc.psum_tensor("q_ps", [P, 4, BANK], F32))

        x_loaded = sem("n1_x_loaded")
        ident_loaded = sem("n1_ident_loaded")
        stats_done = sem("n1_stats_done")
        mean_var_done = sem("n1_mean_var_done")
        var_eps_done = sem("n1_var_eps_done")
        std_done = sem("n1_std_done")
        rstd_done = sem("n1_rstd_done")
        xn_done = sem("n1_xn_done")
        xt_done = sem("n1_xt_done")
        xt_raw_done = sem("n1_xt_raw_done")
        xt_split = sem("n1_xt_split")
        xt_stored = [sem(f"n1_xt_stored{s}") for s in range(2)]
        wq_loaded = [sem(f"q_w_loaded{s}") for s in range(2)]
        wq_hi_done = sem("q_w_hi_done")
        wq_raw_free = sem("q_w_raw_free")
        wq_split = sem("q_w_split")
        wq_free = sem("q_w_free")
        q_ps_free = sem("q_ps_free")
        q_done = sem("q_done")
        q_copied = sem("q_copied")
        q_stored = sem("q_stored")

        block = ctx.enter_context(nc.Block())

        @block.sync
        def _(sp):
            for t in range(NT):
                sp.dma_start(x_sb[:, t, :], x_v[:, t, :]).then_inc(x_loaded, 16)
                if t == 0:
                    sp.dma_start(ident[:], ident_in).then_inc(ident_loaded, 16)
                sp.wait_ge(x_loaded, 16 * (t + 1))
            with sp.Fori(0, NM // 2) as pair:
                m = pair * 2
                for s in range(2):
                    sp.wait_ge(wq_raw_free, m + s + 1)
                    sp.dma_start(wq_raw[:, s, :, :], wq_v[:, :, bass.ds((m + s) * P, P)]).then_inc(wq_loaded[s], 16)

        @block.gpsimd
        def _(pool):
            for t in range(NT):
                pool.wait_ge(xt_raw_done, t + 1)
                pool.dma_start(xt_v[:, :, t * P:(t + 1) * P], xt_raw[:, t % 2, :, :]).then_inc(xt_stored[t % 2], 16)
            with pool.Fori(0, NM // 2) as pair:
                m = pair * 2
                for s in range(2):
                    for half in range(HALVES):
                        pool.wait_ge(q_copied, m * HALVES + s * HALVES + half + 1)
                        pool.dma_start(q_dram[bass.ds((m + s) * P, P), half * BANK:(half + 1) * BANK],
                                       q_sb[:, s * HALVES + half, :]).then_inc(q_stored, 16)
            for s in range(2):
                pool.wait_ge(xt_stored[s], 16 * NT // 2)
            pool.wait_ge(q_stored, 16 * NM * HALVES)

        @block.vector
        def _(dve):
            dve.sem_inc(wq_raw_free, 2)
            for t in range(NT):
                dve.wait_ge(x_loaded, 16 * (t + 1))
                nc.vector.bn_stats(stats[:, t, :], x_sb[:, t, :]).then_inc(stats_done, 1)
                dve.wait_ge(stats_done, t + 1)
                nc.vector.bn_aggr(mean_var[:, t, :], stats[:, t, :]).then_inc(mean_var_done, 1)
            dve.wait_ge(mean_var_done, NT)
            nc.vector.tensor_scalar_add(var_eps[:], mean_var[:, :, 1], EPS).then_inc(var_eps_done, 1)
            dve.wait_ge(std_done, 1)
            nc.vector.reciprocal(rstd[:], std[:]).then_inc(rstd_done, 1)
            dve.wait_ge(rstd_done, 1)

            def split(t):
                dve.wait_ge(xt_raw_done, t + 1)
                nc.vector.tensor_tensor(xt_lo[:, :, t * P:(t + 1) * P], xt_ps[:, t % 2, :, :],
                                        xt_hi[:, :, t * P:(t + 1) * P], ALU.subtract).then_inc(xt_split, 1)

            for t in range(NT):
                if t >= 2:
                    dve.wait_ge(xt_done, t - 1)
                nc.vector.tensor_scalar(xn[:, t % 2, :], x_sb[:, t, :], mean_var[:, t, 0:1], rstd[:, t:t + 1],
                                        ALU.subtract, ALU.mult).then_inc(xn_done, 1)
                if t >= 1:
                    split(t - 1)
            split(NT - 1)
            with dve.Fori(0, NM // 2) as pair:
                m = pair * 2
                for s in range(2):
                    dve.wait_ge(wq_hi_done, m + s + 1)
                    nc.vector.tensor_tensor(wq_lo[:, s, :, :], wq_raw[:, s, :, :], wq_hi[:, s, :, :],
                                            ALU.subtract).then_inc(wq_split, 1)
                    dve.wait_ge(wq_split, m + s + 1)
                    dve.sem_inc(wq_raw_free, 1)

        @block.scalar
        def _(act):
            act.wait_ge(var_eps_done, 1)
            nc.scalar.activation(std[:], var_eps[:], ACT.Sqrt).then_inc(std_done, 1)
            for t in range(NT):
                act.wait_ge(xt_done, t + 1)
                nc.scalar.activation(xt_hi[:, :, t * P:(t + 1) * P], xt_ps[:, t % 2, :, :], ACT.Copy)
                if t >= 2:
                    act.wait_ge(xt_stored[t % 2], 16 * (t // 2))
                nc.scalar.activation(xt_raw[:, t % 2, :, :], xt_ps[:, t % 2, :, :], ACT.Copy).then_inc(xt_raw_done, 1)
            act.sem_inc(q_ps_free, 4)
            with act.Fori(0, NM // 2) as pair:
                m = pair * 2
                for s in range(2):
                    act.wait_ge(wq_loaded[s], m * 8 + 16)
                    act.wait_ge(wq_free, m + s + 1)
                    nc.scalar.activation(wq_hi[:, s, :, :], wq_raw[:, s, :, :], ACT.Copy).then_inc(wq_hi_done, 1)
                    for half in range(HALVES):
                        act.wait_ge(q_done, (m + s) * HALVES + half + 1)
                        nc.scalar.activation(q_sb[:, s * HALVES + half, :], q_ps[:, s * HALVES + half, :],
                                             ACT.Copy).then_inc(q_copied, 1)
                act.wait_ge(q_stored, (m + 2) * HALVES * 16)
                act.sem_inc(q_ps_free, 4)

        @block.tensor
        def _(pe):
            pe.sem_inc(wq_free, 2)
            pe.wait_ge(ident_loaded, 16)
            for t in range(NT):
                pe.wait_ge(xn_done, t + 1)
                if t >= 2:
                    pe.wait_ge(xt_split, t - 1)
                    pe.wait_ge(xt_raw_done, t - 1)
                for c in range(NC):
                    last = nc.tensor.transpose(xt_ps[:, t % 2, c, :], xn[:, t % 2, c * P:(c + 1) * P], ident[:])
                last.then_inc(xt_done, 1)
            pe.wait_ge(xt_split, NT)
            with pe.Fori(0, NM // 2) as pair:
                m = pair * 2
                for s in range(2):
                    pe.wait_ge(wq_split, m + s + 1)
                    for half in range(HALVES):
                        pe.wait_ge(q_ps_free, (m + s) * HALVES + half + 1)
                        cols = slice(half * BANK, (half + 1) * BANK)
                        split_product(nc, q_ps[:, s * HALVES + half, :],
                                      [(wq_hi[:, s, c, :], wq_lo[:, s, c, :], xt_hi[:, c, cols], xt_lo[:, c, cols])
                                       for c in range(NC)]).then_inc(q_done, 1)
                    pe.wait_ge(q_done, (m + s + 1) * HALVES)
                    pe.sem_inc(wq_free, 1)


def attention(nc, ctx_t, wk, wv, ident_in, xt_dram, q_dram, l_dram, o_dram, B, KV, HD, G, Q):
    CTX = ctx_t.shape[2]
    D = ctx_t.shape[1]
    NC = D // P
    S = CTX + Q
    CW = 3 * P
    CHUNKS = [(s0, min(CW, S - s0)) for s0 in range(0, S, CW)]
    TILES = [(s0, min(P, S - s0)) for s0 in range(0, S, P)]
    NCH, NTL = len(CHUNKS), len(TILES)
    SE = S + S % 2
    GQ = G * Q
    NJ = GQ // P
    QS = G * HD
    R = HD + 1
    SCALE = float(HD) ** -0.5
    KVD = KV * HD
    HV = GQ // BANK
    NG = KV * NTL
    NPR = KV * NCH + NTL
    NJB = NJ * NCH
    JOBS_AT, JOBS_PER = 2, 4
    M_AT = JOBS_AT + NJB // JOBS_PER
    NORM_AT = 7
    ONE = 1
    assert KVD == CW and GQ == 2 * BANK and NG % 6 == 0 and NJB % 2 == 0 and M_AT < NTL - 1

    wk_v = wk.rearrange("(c p) m -> p c m", p=P)
    wv_v = wv.rearrange("(c p) m -> p c m", p=P)
    ctx_v = ctx_t.rearrange("b (c p) s -> p (b c) s", p=P)
    xt_v = xt_dram.rearrange("(c p) t -> p c t", p=P)
    q_v = q_dram.rearrange("(h d) t -> d h t", d=HD)
    o_v = o_dram.rearrange("(h d) t -> d h t", d=HD)
    l_v = l_dram.rearrange("(o h) t -> o h t", o=1)

    with ExitStack() as ctx:
        def sb(name, shape, dt=F32):
            return ctx.enter_context(nc.sbuf_tensor(name, shape, dt))

        def pb(name, shape):
            return ctx.enter_context(nc.psum_tensor(name, shape, F32))

        def sem(name):
            return ctx.enter_context(nc.semaphore(name))

        ident = sb("a_ident", [P, P])
        wk_hi = sb("a_wk_hi", [P, NC, KVD], F32R)
        wk_lo = sb("a_wk_lo", [P, NC, KVD], F32R)
        wv_hi = sb("a_wv_hi", [P, NC, KVD], F32R)
        wv_lo = sb("a_wv_lo", [P, NC, KVD], F32R)
        kt_hi = sb("a_kt_hi", [R, KV, SE], F32R)
        kt_lo = sb("a_kt_lo", [R, KV, SE], F32R)
        v_hi = sb("a_v_hi", [P, NTL, KV, R], F32R)
        v_lo = sb("a_v_lo", [P, NTL, KV, R], F32R)
        work = sb("a_work", [P, 2, 3 * GQ], F32R)
        h_raw = sb("a_h_raw", [P, 2, NC, CW])
        q_raw = sb("a_q_raw", [HD, G, Q])
        q_hi = sb("a_q_hi", [R, 2, GQ], F32R)
        q_lo = sb("a_q_lo", [HD, 2, GQ], F32R)
        o_sb = sb("a_o_sb", [R, GQ])
        l_bc = sb("a_l_bc", [HD, GQ])
        m_part = sb("a_m_part", [P, NJ, NCH])
        m_all = sb("a_m_all", [P, NJ])
        m_row = sb("a_m_row", [NJ, P], F32R)
        s_ps = pb("a_s_ps", [P, 2, HV, BANK])
        o_ps = pb("a_o_ps", [P, HV, BANK])
        m_ps = pb("a_m_ps", [P, 2, BANK])
        pr_ps = [s_ps[:, n // 2, n % 2, :] for n in range(4)]

        def h_at(part, c):
            return work[:, part, c % 2 * NC * CW:(c % 2 + 1) * NC * CW].rearrange("p (c s) -> p c s", c=NC)

        def p_at(part, g):
            return work[:, part, g % 3 * GQ:(g % 3 + 1) * GQ]

        w_loaded = sem("a_w_loaded")
        w_hi_done = sem("a_w_hi_done")
        w_split = sem("a_w_split")
        ones_set = sem("a_ones_set")
        h_loaded = [sem(f"a_h_loaded{s}") for s in range(2)]
        h_hi_done = sem("a_h_hi_done")
        h_split = sem("a_h_split")
        pr_done = sem("a_pr_done")
        pr_hi_done = sem("a_pr_hi_done")
        pr_split = sem("a_pr_split")
        q_loaded = sem("a_q_loaded")
        q_hi_done = sem("a_q_hi_done")
        q_split = sem("a_q_split")
        mm_done = sem("a_mm_done")
        mm_reduced = sem("a_mm_reduced")
        m_all_done = sem("a_m_all_done")
        m_turned = sem("a_m_turned")
        m_row_done = sem("a_m_row_done")
        m_row_placed = sem("a_m_row_placed")
        s_done = sem("a_s_done")
        exp_done = sem("a_exp_done")
        p_split = sem("a_p_split")
        pv_done = sem("a_pv_done")
        o_copied = sem("a_o_copied")
        l_stored = sem("a_l_stored")
        l_spread = sem("a_l_spread")
        l_inverted = sem("a_l_inverted")
        o_normed = sem("a_o_normed")
        o_stored = sem("a_o_stored")
        o_sb_free = sem("a_o_sb_free")

        def jobs_of(g):
            kv, t = divmod(g, NTL)
            if kv + 1 >= KV or not JOBS_AT <= t < M_AT:
                return []
            n0 = (t - JOBS_AT) * JOBS_PER
            return [(kv + 1, n) for n in range(n0, n0 + JOBS_PER)]

        def first_jobs(c):
            return [(0, c * NJ + j) for j in range(NJ)]

        def plan_of(c):
            vs = [("v", 3 * c + i) for i in range(3)]
            js = [("job", n) for n in first_jobs(c)]
            if c == NCH - 1:
                return js + [("m_all", 0)] + vs[:1] + [("m", 0)] + vs[1:]
            return vs[:1] + js[:3] + vs[1:2] + js[3:6] + vs[2:] + js[6:]

        def k_index(c, kv):
            return 7 * c + kv

        def v_index(t):
            return 7 * (t // 3) + KV + t % 3

        block = ctx.enter_context(nc.Block())

        @block.gpsimd
        def _(pool):
            pool.wait_ge(w_split, 2)
            with pool.Fori(0, B) as b:
                def load_q(kv):
                    pool.wait_ge(q_split, ONE + b * KV + kv)
                    pool.dma_start(q_raw[:], q_v[:, kv * G:(kv + 1) * G, bass.ds(b * Q, Q)]).then_inc(q_loaded, 16)

                load_q(0)
                for c, (s0, w) in enumerate(CHUNKS):
                    pool.wait_ge(h_split, ONE + b * NCH + (c - 1 if c >= 2 else 0))
                    wc = min(w, CTX - s0)
                    pool.dma_start(h_raw[:, c % 2, :, 0:wc], ctx_v[:, bass.ds(b * NC, NC), s0:s0 + wc]).then_inc(h_loaded[c % 2], 16)
                    if wc < w:
                        pool.dma_start(h_raw[:, c % 2, :, wc:w], xt_v[:, :, bass.ds(b * Q, Q)]).then_inc(h_loaded[c % 2], 16)
                for kv in range(1, KV):
                    load_q(kv)

        @block.sync
        def _(sp):
            sp.dma_start(ident[:], ident_in).then_inc(w_loaded, 16)
            sp.wait_ge(w_loaded, 16)
            sp.dma_start(h_raw[:, 0, :, :], wk_v).then_inc(w_loaded, 16)
            sp.wait_ge(w_loaded, 32)
            sp.dma_start(h_raw[:, 1, :, :], wv_v).then_inc(w_loaded, 16)
            sp.sem_inc(o_sb_free, ONE)
            with sp.Fori(0, B) as b:
                def place_m(kv):
                    sp.wait_ge(m_row_done, b * KV + kv + 1)
                    sp.dma_start(q_hi[HD:R, kv % 2, :].bitcast(F32).rearrange("o (j t) -> o j t", j=NJ), m_row[:].bitcast(F32)).then_inc(m_row_placed, 16)

                place_m(0)
                for kv in range(KV):
                    if kv + 1 < KV:
                        place_m(kv + 1)
                    sp.wait_ge(o_copied, ONE + b * KV + kv + 1)
                    sp.dma_start(l_v[:, kv, :], o_sb[HD:R, :]).then_inc(l_stored, 16)
                    sp.wait_ge(l_stored, (b * KV + kv + 1) * 16)
                    sp.dma_start(l_bc[:], l_dram[kv, :].partition_broadcast(HD)).then_inc(l_spread, 16)
                    sp.wait_ge(o_normed, b * KV + kv + 1)
                    sp.dma_start(o_v[:, kv * G:(kv + 1) * G, bass.ds(b * Q, Q)],
                                 o_sb[0:HD, :].rearrange("d (g q) -> d g q", g=G)).then_inc(o_stored, 16)
                    sp.wait_ge(o_stored, (b * KV + kv + 1) * 16)
                    sp.sem_inc(o_sb_free, 1)

        @block.scalar
        def _(act):
            for n, hi in enumerate((wk_hi, wv_hi)):
                act.wait_ge(w_loaded, 16 * (n + 2))
                nc.scalar.activation(hi[:], h_raw[:, n, :, :], ACT.Copy).then_inc(w_hi_done, 1)
            act.sem_inc(o_copied, ONE)
            with act.Fori(0, B) as b:
                def split_q(kv):
                    act.wait_ge(q_loaded, (b * KV + kv + 1) * 16)
                    nc.scalar.activation(q_hi[0:HD, kv % 2, :], q_raw[:].rearrange("d g q -> d (g q)"),
                                         ACT.Copy).then_inc(q_hi_done, 1)

                def split_h(c):
                    if c >= 2:
                        act.wait_ge(pr_done, b * NPR + 7 * (c - 1))
                    per = (64, 32)[c % 2]
                    act.wait_ge(h_loaded[c % 2], b * per + (16 * (c // 2 + 1) if c < NCH - 1 else per))
                    w = CHUNKS[c][1]
                    w += w % 2
                    nc.scalar.activation(h_at(0, c)[:, :, 0:w], h_raw[:, c % 2, :, 0:w], ACT.Copy).then_inc(h_hi_done, 1)

                def evac(n, dst, src):
                    act.wait_ge(pr_done, b * NPR + n + 1)
                    nc.scalar.activation(dst, src, ACT.Copy).then_inc(pr_hi_done, 1)

                def copy_o(kv):
                    act.wait_ge(pv_done, ONE + b * NG + (kv + 1) * NTL)
                    act.wait_ge(o_sb_free, ONE + b * KV + kv)
                    nc.scalar.activation(o_sb[:], o_ps[0:R, :, :].rearrange("p a n -> p (a n)"), ACT.Copy).then_inc(o_copied, 1)

                act.wait_ge(pv_done, ONE + b * NG)
                split_q(0)
                split_h(0)
                split_h(1)
                for c, (s0, w) in enumerate(CHUNKS):
                    w += w % 2
                    for kv in range(KV):
                        n = k_index(c, kv)
                        evac(n, kt_hi[0:HD, kv, s0:s0 + w], pr_ps[n % 4][0:HD, 0:w])
                    for t in range(3 * c, 3 * c + 3):
                        n, m = v_index(t), TILES[t][1]
                        evac(n, v_hi[0:m, t, :, 0:HD], pr_ps[n % 4][0:m, 0:KVD].rearrange("p (k d) -> p k d", k=KV))
                    if c + 2 < NCH:
                        split_h(c + 2)
                for g in range(NG):
                    kv, t = divmod(g, NTL)
                    m = TILES[t][1]
                    act.wait_ge(s_done, b * NG + g + 1)
                    if g >= 3:
                        act.wait_ge(pv_done, ONE + b * NG + g - 2)
                    s_in = s_ps[0:m, g % 2, :, :].rearrange("p a n -> p (a n)")
                    nc.scalar.activation(p_at(0, g)[0:m, :], s_in, ACT.Exp, scale=SCALE)
                    nc.scalar.activation(s_in, s_in, ACT.Exp, scale=SCALE).then_inc(exp_done, 1)
                    if t == 0 and kv + 1 < KV:
                        split_q(kv + 1)
                    if t == 1 and kv > 0:
                        copy_o(kv - 1)
                copy_o(KV - 1)

        @block.vector
        def _(dve):
            for n, (hi, lo) in enumerate(((wk_hi, wk_lo), (wv_hi, wv_lo))):
                dve.wait_ge(w_hi_done, n + 1)
                nc.vector.tensor_tensor(lo[:], h_raw[:, n, :, :], hi[:], ALU.subtract).then_inc(w_split, 1)
            nc.vector.memset(kt_hi[HD:R, :, :].bitcast(F32), 1.0).then_inc(ones_set, 1)
            nc.vector.memset(v_hi[:, :, :, HD:R].bitcast(F32), 1.0).then_inc(ones_set, 1)
            nc.vector.memset(v_lo[:, :, :, HD:R].bitcast(F32), 0.0).then_inc(ones_set, 1)
            dve.sem_inc(q_split, ONE)
            dve.sem_inc(h_split, ONE)
            dve.sem_inc(mm_reduced, ONE)
            with dve.Fori(0, B) as b:
                def split_q(kv):
                    dve.wait_ge(q_hi_done, b * KV + kv + 1)
                    nc.vector.tensor_tensor(q_lo[:, kv % 2, :], q_raw[:].rearrange("d g q -> d (g q)"),
                                            q_hi[0:HD, kv % 2, :], ALU.subtract).then_inc(q_split, 1)

                def split_h(c):
                    dve.wait_ge(h_hi_done, b * NCH + c + 1)
                    w = CHUNKS[c][1]
                    w += w % 2
                    nc.vector.tensor_tensor(h_at(1, c)[:, :, 0:w], h_raw[:, c % 2, :, 0:w], h_at(0, c)[:, :, 0:w],
                                            ALU.subtract).then_inc(h_split, 1)

                def evac(n, dst, src, hi):
                    dve.wait_ge(pr_hi_done, b * NPR + n + 1)
                    nc.vector.tensor_tensor(dst, src, hi, ALU.subtract).then_inc(pr_split, 1)

                def reduce_job(kv, n):
                    c, j = divmod(n, NJ)
                    dve.wait_ge(mm_done, b * KV * NJB + kv * NJB + n + 1)
                    nc.vector.reduce_max(m_part[:, j, c:c + 1], m_ps[:, n % 2, 0:CHUNKS[c][1]], AX_X).then_inc(mm_reduced, 1)

                def join_m(kv):
                    dve.wait_ge(mm_reduced, ONE + b * KV * NJB + (kv + 1) * NJB)
                    nc.vector.reduce_max(m_all[:], m_part[:], AX_X).then_inc(m_all_done, 1)

                def finish_m(kv):
                    dve.wait_ge(m_turned, b * KV + kv + 1)
                    nc.vector.tensor_scalar(m_row[:], m_ps[0:NJ, 0, 0:P], -1.0, None, ALU.mult).then_inc(m_row_done, 1)

                def split_p(g):
                    m = TILES[g % NTL][1]
                    dve.wait_ge(exp_done, b * NG + g + 1)
                    nc.vector.tensor_tensor(p_at(1, g)[0:m, :], s_ps[0:m, g % 2, :, :].rearrange("p a n -> p (a n)"),
                                            p_at(0, g)[0:m, :], ALU.subtract).then_inc(p_split, 1)

                def norm(kv):
                    dve.wait_ge(l_spread, (b * KV + kv + 1) * 16)
                    nc.vector.reciprocal(l_bc[:], l_bc[:]).then_inc(l_inverted, 1)
                    dve.wait_ge(l_inverted, b * KV + kv + 1)
                    nc.vector.tensor_tensor(o_sb[0:HD, :], o_sb[0:HD, :], l_bc[:], ALU.mult).then_inc(o_normed, 1)

                split_q(0)
                split_h(0)
                split_h(1)
                for c, (s0, w) in enumerate(CHUNKS):
                    w += w % 2
                    for kv in range(KV):
                        n = k_index(c, kv)
                        evac(n, kt_lo[0:HD, kv, s0:s0 + w], pr_ps[n % 4][0:HD, 0:w], kt_hi[0:HD, kv, s0:s0 + w])
                    for what, n in plan_of(c):
                        if what == "job":
                            reduce_job(*n)
                        elif what == "v":
                            m = TILES[n][1]
                            i = v_index(n)
                            evac(i, v_lo[0:m, n, :, 0:HD], pr_ps[i % 4][0:m, 0:KVD].rearrange("p (k d) -> p k d", k=KV),
                                 v_hi[0:m, n, :, 0:HD])
                        elif what == "m_all":
                            join_m(n)
                        else:
                            finish_m(n)
                    if c + 2 < NCH:
                        split_h(c + 2)
                for g in range(NG + 1):
                    kv, t = divmod(g, NTL)
                    if g >= 1:
                        split_p(g - 1)
                    if t == 1 and kv + 1 < KV:
                        split_q(kv + 1)
                    if t == NORM_AT and kv > 0:
                        norm(kv - 1)
                    for job in jobs_of(g):
                        reduce_job(*job)
                    if t == M_AT and kv + 1 < KV:
                        join_m(kv + 1)
                        finish_m(kv + 1)
                norm(KV - 1)

        @block.tensor
        def _(pe):
            pe.wait_ge(w_loaded, 48)
            pe.wait_ge(w_split, 2)
            pe.wait_ge(ones_set, 3)
            pe.sem_inc(pv_done, ONE)
            with pe.Fori(0, B) as b:
                def project_k(c, kv):
                    n, w = k_index(c, kv), CHUNKS[c][1]
                    w += w % 2
                    if n >= 4:
                        pe.wait_ge(pr_split, b * NPR + n - 3)
                    rows = slice(kv * HD, (kv + 1) * HD)
                    split_product(nc, pr_ps[n % 4][0:HD, 0:w],
                                  [(wk_hi[:, i, rows], wk_lo[:, i, rows], h_at(0, c)[:, i, 0:w], h_at(1, c)[:, i, 0:w])
                                   for i in range(NC)]).then_inc(pr_done, 1)

                def project_v(t):
                    n, m = v_index(t), TILES[t][1]
                    s0 = t % 3 * P
                    pe.wait_ge(pr_split, b * NPR + n - 3)
                    split_product(nc, pr_ps[n % 4][0:m, 0:KVD],
                                  [(h_at(0, t // 3)[:, i, s0:s0 + m], h_at(1, t // 3)[:, i, s0:s0 + m], wv_hi[:, i, :], wv_lo[:, i, :])
                                   for i in range(NC)]).then_inc(pr_done, 1)

                def job(kv, n):
                    c, j = divmod(n, NJ)
                    s0, w = CHUNKS[c]
                    w += w % 2
                    if kv > 0 or n >= 2:
                        pe.wait_ge(mm_reduced, ONE + b * KV * NJB + kv * NJB + n - 1)
                    nc.tensor.matmul(m_ps[:, n % 2, 0:w], q_hi[0:HD, kv % 2, j * P:(j + 1) * P], kt_hi[0:HD, kv, s0:s0 + w],
                                     start=True, stop=True).then_inc(mm_done, 1)

                def turn_m(kv):
                    pe.wait_ge(m_all_done, b * KV + kv + 1)
                    nc.tensor.transpose(m_ps[0:NJ, 0, 0:P], m_all[:], ident[:]).then_inc(m_turned, 1)

                def scores(g, half):
                    kv, t = divmod(g, NTL)
                    s0, m = TILES[t]
                    keys = slice(s0, s0 + m)
                    cols = slice(half * BANK, (half + 1) * BANK)
                    out = s_ps[0:m, g % 2, half, :]
                    nc.tensor.matmul(out, kt_hi[0:R, kv, keys], q_hi[0:R, kv % 2, cols], start=True, stop=False)
                    nc.tensor.matmul(out, kt_hi[0:HD, kv, keys], q_lo[0:HD, kv % 2, cols], start=False, stop=False)
                    return nc.tensor.matmul(out, kt_lo[0:HD, kv, keys], q_hi[0:HD, kv % 2, cols], start=False, stop=True)

                def values(g, half):
                    kv, t = divmod(g, NTL)
                    m = TILES[t][1]
                    cols = slice(half * BANK, (half + 1) * BANK)
                    pairs = three_passes(v_hi[0:m, t, kv, :], v_lo[0:m, t, kv, :], p_at(0, g)[0:m, cols], p_at(1, g)[0:m, cols])
                    for n, (stationary, moving) in enumerate(pairs):
                        last = nc.tensor.matmul(o_ps[0:R, half, :], stationary, moving,
                                                start=(t == 0 and n == 0), stop=(t == NTL - 1 and n == 2))
                    return last

                for c in range(NCH):
                    pe.wait_ge(h_split, ONE + b * NCH + c + 1)
                    for kv in range(KV):
                        project_k(c, kv)
                    for i, (what, n) in enumerate(plan_of(c)):
                        if what == "job":
                            if n[1] % NJ == 0:
                                pe.wait_ge(q_split, ONE + b * KV + 1)
                                pe.wait_ge(pr_split, b * NPR + k_index(c, 0) + 1)
                            job(*n)
                        elif what == "v":
                            project_v(n)
                        elif what == "m":
                            turn_m(n)
                pe.wait_ge(pr_split, (b + 1) * NPR)
                for g in range(NG + 2):
                    kv, t = divmod(g, NTL)
                    after = list(jobs_of(g))
                    if after and t == JOBS_AT:
                        pe.wait_ge(q_split, ONE + b * KV + kv + 2)
                    if g < NG:
                        if t == 0:
                            pe.wait_ge(m_row_placed, (b * KV + kv + 1) * 16)
                            pe.wait_ge(q_split, ONE + b * KV + kv + 1)
                        if g >= 2:
                            pe.wait_ge(p_split, b * NG + g - 1)
                        scores(g, 0)
                        if after:
                            job(*after.pop(0))
                        scores(g, 1).then_inc(s_done, 1)
                        if t == M_AT and kv + 1 < KV:
                            turn_m(kv + 1)
                        if after:
                            job(*after.pop(0))
                    if g >= 2:
                        if g >= NG:
                            pe.wait_ge(p_split, b * NG + g - 1)
                        if (g - 2) % NTL == 0 and g > 2:
                            pe.wait_ge(o_copied, ONE + b * KV + kv)
                        if g == 2:
                            pe.wait_ge(o_copied, ONE + b * KV)
                        values(g - 2, 0)
                        if after:
                            job(*after.pop(0))
                        values(g - 2, 1).then_inc(pv_done, 1)
                        if after:
                            job(*after.pop(0))


def output_and_router(nc, x, wo, wg, bg, earlier_in, ident_in, o_dram, x1, x2_hi, x2_lo, weight):
    T, D = x.shape
    QD = wo.shape[0]
    E = wg.shape[1]
    NT, NC, NK = T // P, D // P, QD // P
    PARTS = 4
    KP = NK // PARTS
    x_v = x.rearrange("(t p) d -> p t d", p=P)
    wo_v = wo.rearrange("(k p) d -> p k d", p=P)
    o_v = o_dram.rearrange("(k p) t -> p k t", p=P)

    with ExitStack() as ctx:
        def sb(name, shape, dt=F32):
            return ctx.enter_context(nc.sbuf_tensor(name, shape, dt))

        def pb(name, shape):
            return ctx.enter_context(nc.psum_tensor(name, shape, F32))

        def sem(name):
            return ctx.enter_context(nc.semaphore(name))

        ident = sb("o_ident", [P, P])
        wg_sb = sb("o_wg", [P, NC, E])
        bg_bc = sb("o_bg", [P, E])
        earlier = sb("o_earlier", [P, E, E])
        wo_raw = sb("o_w_raw", [P, NK, D])
        wo_hi = sb("o_w_hi", [P, NK, D], F32R)
        wo_lo = sb("o_w_lo", [P, NK, D], F32R)
        o_raw = sb("o_raw", [P, 2, NK, P])
        o_hi = sb("o_hi", [P, 2, NK, P], F32R)
        o_lo = sb("o_lo", [P, 2, NK, P], F32R)
        x_sb = sb("o_x", [P, 2, D])
        stats = sb("o_stats", [P, NT * 6])
        mean_var = sb("o_mean_var", [P, NT * 2])
        var_eps = sb("o_var_eps", [P, NT])
        std = sb("o_std", [P, NT])
        rstd = sb("o_rstd", [P, NT])
        xn = sb("o_xn", [P, 2, D])
        x2_raw = sb("o_x2_raw", [P, 2, NC, P])
        logits = sb("o_logits", [P, NT * E])
        above = sb("o_above", [P, NT, E, E])
        same = sb("o_same", [P, NT, E, E])
        rank = sb("o_rank", [P, NT, E])
        y_ps = pb("o_y_ps", [P, 2, BANK])
        x2_ps = pb("o_x2_ps", [P, 2, NC, P])
        g_ps = pb("o_g_ps", [P, 2, BANK])

        const_loaded = sem("o_const_loaded")
        wo_loaded = [sem(f"o_w_loaded{n}") for n in range(PARTS)]
        wo_hi_done = sem("o_w_hi_done")
        wo_split = sem("o_w_split")
        o_loaded = [sem(f"o_loaded{s}") for s in range(2)]
        o_raw_free = sem("o_raw_free")
        o_hi_done = sem("o_hi_done")
        o_split = sem("o_split")
        o_free = sem("o_free")
        y_free = sem("o_y_free")
        y_done = sem("o_y_done")
        x1_done = sem("o_x1_done")
        stats_done = sem("o_stats_done")
        mean_var_done = sem("o_mean_var_done")
        var_eps_done = sem("o_var_eps_done")
        std_done = sem("o_std_done")
        rstd_done = sem("o_rstd_done")
        xn_free = sem("o_xn_free")
        xn_done = sem("o_xn_done")
        x2_ps_free = sem("o_x2_ps_free")
        x2_turned = sem("o_x2_turned")
        x2_raw_free = sem("o_x2_raw_free")
        x2_raw_done = sem("o_x2_raw_done")
        x2_split = sem("o_x2_split")
        g_done = sem("o_g_done")
        logits_done = sem("o_logits_done")
        rank_step = sem("o_rank_step")
        weight_done = sem("o_weight_done")

        block = ctx.enter_context(nc.Block())

        @block.sync
        def _(sp):
            sp.dma_start(ident[:], ident_in).then_inc(const_loaded, 16)
            sp.dma_start(wg_sb[:], wg.rearrange("(c p) e -> p c e", p=P)).then_inc(const_loaded, 16)
            sp.dma_start(bg_bc[:], bg.partition_broadcast(P)).then_inc(const_loaded, 16)
            sp.dma_start(earlier[:], earlier_in.rearrange("p (e j) -> p e j", e=E)).then_inc(const_loaded, 16)
            with sp.Fori(0, NT // 2) as pair:
                i = pair * 2
                for s in range(2):
                    sp.wait_ge(o_raw_free, i + s + 1)
                    sp.dma_start(o_raw[:, s, :, :], o_v[:, :, bass.ds((i + s) * P, P)]).then_inc(o_loaded[s], 16)
                    sp.dma_start(x_sb[:, s, :], x[bass.ds((i + s) * P, P), :]).then_inc(o_loaded[s], 16)

        @block.gpsimd
        def _(pool):
            for n in range(PARTS):
                part = slice(n * KP, (n + 1) * KP)
                pool.dma_start(wo_raw[:, part, :], wo_v[:, part, :]).then_inc(wo_loaded[n], 16)

        @block.scalar
        def _(act):
            for n in range(PARTS):
                part = slice(n * KP, (n + 1) * KP)
                act.wait_ge(wo_loaded[n], 16)
                nc.scalar.activation(wo_hi[:, part, :], wo_raw[:, part, :], ACT.Copy).then_inc(wo_hi_done, 1)
            with act.Fori(0, NT // 2) as pair:
                i = pair * 2
                for s in range(2):
                    act.wait_ge(o_loaded[s], i * 16 + 32)
                    act.wait_ge(o_free, i + s + 1)
                    nc.scalar.activation(o_hi[:, s, :, :], o_raw[:, s, :, :], ACT.Copy).then_inc(o_hi_done, 1)
            act.wait_ge(var_eps_done, 1)
            nc.scalar.activation(std[:], var_eps[:], ACT.Sqrt).then_inc(std_done, 1)
            with act.Fori(0, NT // 2) as pair:
                i = pair * 2
                for s in range(2):
                    act.wait_ge(x2_turned, i + s + 1)
                    nc.scalar.activation(x2_hi[:, :, bass.ds((i + s) * P, P)], x2_ps[:, s, :, :], ACT.Copy)
                    act.wait_ge(x2_raw_free, i + s + 1)
                    nc.scalar.activation(x2_raw[:, s, :, :], x2_ps[:, s, :, :], ACT.Copy).then_inc(x2_raw_done, 1)

        @block.vector
        def _(dve):
            dve.sem_inc(o_raw_free, 2)
            dve.sem_inc(y_free, 2)
            dve.sem_inc(x2_ps_free, 2)
            for n in range(PARTS):
                part = slice(n * KP, (n + 1) * KP)
                dve.wait_ge(wo_hi_done, n + 1)
                nc.vector.tensor_tensor(wo_lo[:, part, :], wo_raw[:, part, :], wo_hi[:, part, :], ALU.subtract).then_inc(wo_split, 1)
            with dve.Fori(0, NT // 2) as pair:
                i = pair * 2
                for s in range(2):
                    dve.wait_ge(o_hi_done, i + s + 1)
                    nc.vector.tensor_tensor(o_lo[:, s, :, :], o_raw[:, s, :, :], o_hi[:, s, :, :], ALU.subtract).then_inc(o_split, 1)
                for s in range(2):
                    dve.wait_ge(y_done, i + s + 1)
                    nc.vector.tensor_tensor(x1[:, bass.ds((i + s) * D, D)], y_ps[:, s, :], x_sb[:, s, :], ALU.add).then_inc(x1_done, 1)
                    dve.wait_ge(x1_done, i + s + 1)
                    dve.sem_inc(y_free, 1)
                    dve.sem_inc(o_raw_free, 1)
                    nc.vector.bn_stats(stats[:, bass.ds((i + s) * 6, 6)], x1[:, bass.ds((i + s) * D, D)]).then_inc(stats_done, 1)
            dve.wait_ge(stats_done, NT)
            for t in range(NT):
                nc.vector.bn_aggr(mean_var[:, 2 * t:2 * t + 2], stats[:, 6 * t:6 * t + 6]).then_inc(mean_var_done, 1)
            dve.wait_ge(mean_var_done, NT)
            nc.vector.tensor_scalar_add(var_eps[:], mean_var[:].rearrange("p (t k) -> p t k", k=2)[:, :, 1], EPS).then_inc(var_eps_done, 1)
            dve.wait_ge(std_done, 1)
            nc.vector.reciprocal(rstd[:], std[:]).then_inc(rstd_done, 1)
            dve.wait_ge(rstd_done, 1)
            dve.wait_ge(const_loaded, 64)
            with dve.Fori(0, NT // 2) as pair:
                i = pair * 2
                for s in range(2):
                    dve.wait_ge(xn_free, i + s + 1)
                    nc.vector.tensor_scalar(xn[:, s, :], x1[:, bass.ds((i + s) * D, D)], mean_var[:, bass.ds((i + s) * 2, 1)],
                                            rstd[:, bass.ds(i + s, 1)], ALU.subtract, ALU.mult).then_inc(xn_done, 1)
                for s in range(2):
                    dve.wait_ge(x2_raw_done, i + s + 1)
                    cols = bass.ds((i + s) * P, P)
                    nc.vector.tensor_tensor(x2_lo[:, :, cols], x2_ps[:, s, :, :], x2_hi[:, :, cols], ALU.subtract).then_inc(x2_split, 1)
                    dve.wait_ge(x2_split, i + s + 1)
                    dve.sem_inc(x2_ps_free, 1)
                for s in range(2):
                    dve.wait_ge(g_done, i + s + 1)
                    nc.vector.tensor_tensor(logits[:, bass.ds((i + s) * E, E)], g_ps[:, s, 0:E], bg_bc[:], ALU.add).then_inc(logits_done, 1)
            dve.wait_ge(logits_done, NT)
            of_other = logits[:].rearrange("p (t o j) -> p t o j", o=1, j=E).to_broadcast([P, NT, E, E])
            of_this = logits[:].rearrange("p (t e o) -> p t e o", o=1, e=E).to_broadcast([P, NT, E, E])
            nc.vector.tensor_tensor(above[:], of_other, of_this, ALU.is_gt).then_inc(rank_step, 1)
            nc.vector.tensor_tensor(same[:], of_other, of_this, ALU.is_equal).then_inc(rank_step, 1)
            dve.wait_ge(rank_step, 2)
            before = earlier[:].rearrange("p (o e) j -> p o e j", o=1).to_broadcast([P, NT, E, E])
            nc.vector.tensor_tensor(same[:], same[:], before, ALU.mult).then_inc(rank_step, 1)
            dve.wait_ge(rank_step, 3)
            nc.vector.tensor_tensor(above[:], above[:], same[:], ALU.add).then_inc(rank_step, 1)
            dve.wait_ge(rank_step, 4)
            nc.vector.reduce_sum(rank[:], above[:], AX_X).then_inc(rank_step, 1)
            dve.wait_ge(rank_step, 5)
            nc.vector.tensor_scalar(weight[:], rank[:].rearrange("p t e -> p (t e)"), TOP_K - 0.5, 1.0 / TOP_K,
                                    ALU.is_lt, ALU.mult).then_inc(weight_done, 1)
            dve.wait_ge(weight_done, 1)

        @block.tensor
        def _(pe):
            pe.sem_inc(o_free, 2)
            pe.sem_inc(xn_free, 2)
            pe.sem_inc(x2_raw_free, 2)
            pe.wait_ge(wo_split, PARTS)
            with pe.Fori(0, NT // 2) as pair:
                i = pair * 2
                for s in range(2):
                    pe.wait_ge(o_split, i + s + 1)
                    pe.wait_ge(y_free, i + s + 1)
                    split_product(nc, y_ps[:, s, :], [(o_hi[:, s, k, :], o_lo[:, s, k, :], wo_hi[:, k, :], wo_lo[:, k, :])
                                                      for k in range(NK)]).then_inc(y_done, 1)
                pe.wait_ge(y_done, i + 2)
                pe.sem_inc(o_free, 2)
            pe.wait_ge(const_loaded, 64)
            with pe.Fori(0, NT // 2) as pair:
                i = pair * 2
                for s in range(2):
                    pe.wait_ge(xn_done, i + s + 1)
                    pe.wait_ge(x2_ps_free, i + s + 1)
                    for c in range(NC):
                        last = nc.tensor.transpose(x2_ps[:, s, c, :], xn[:, s, c * P:(c + 1) * P], ident[:])
                    last.then_inc(x2_turned, 1)
                pe.wait_ge(x2_turned, i + 2)
                pe.sem_inc(xn_free, 2)
                for s in range(2):
                    pe.wait_ge(x2_raw_done, i + s + 1)
                    for c in range(NC):
                        last = nc.tensor.matmul(g_ps[:, s, 0:E], x2_raw[:, s, c, :], wg_sb[:, c, :], start=(c == 0), stop=(c == NC - 1))
                    last.then_inc(g_done, 1)
                pe.wait_ge(g_done, i + 2)
                pe.sem_inc(x2_raw_free, 2)


def experts(nc, we, be, out, x1, x2_hi, x2_lo, weight):
    E, D, H = we.shape
    T = out.shape[0]
    NT, NC = T // P, D // P
    we_v = we.rearrange("e (c p) h -> p (e c) h", p=P)
    out_v = out.rearrange("(t p) h -> p t h", p=P)

    with ExitStack() as ctx:
        def sb(name, shape, dt=F32):
            return ctx.enter_context(nc.sbuf_tensor(name, shape, dt))

        def sem(name):
            return ctx.enter_context(nc.semaphore(name))

        w_raw = sb("e_w_raw", [P, 2, NC, H])
        w_hi = sb("e_w_hi", [P, 2, NC, H], F32R)
        w_lo = sb("e_w_lo", [P, 2, NC, H], F32R)
        b_bc = sb("e_b", [P, 2, H])
        z = sb("e_z", [P, 2, H])
        r = sb("e_r", [P, 2, H])
        y_ps = ctx.enter_context(nc.psum_tensor("e_y_ps", [P, NT, BANK], F32))

        w_loaded = [sem(f"e_w_loaded{s}") for s in range(2)]
        b_loaded = [sem(f"e_b_loaded{s}") for s in range(2)]
        w_raw_free = sem("e_w_raw_free")
        b_free = sem("e_b_free")
        w_hi_done = sem("e_w_hi_done")
        w_split = sem("e_w_split")
        w_free = sem("e_w_free")
        y_free = sem("e_y_free")
        y_done = sem("e_y_done")
        z_free = sem("e_z_free")
        z_done = sem("e_z_done")
        r_free = sem("e_r_free")
        r_done = sem("e_r_done")
        added = sem("e_added")
        stored = sem("e_stored")

        block = ctx.enter_context(nc.Block())

        @block.sync
        def _(sp):
            with sp.Fori(0, E // 2) as pair:
                e = pair * 2
                for s in range(2):
                    sp.wait_ge(w_raw_free, e + s + 1)
                    sp.dma_start(w_raw[:, s, :, :], we_v[:, bass.ds((e + s) * NC, NC), :]).then_inc(w_loaded[s], 16)
                    sp.wait_ge(b_free, e + s + 1)
                    sp.dma_start(b_bc[:, s, :], be[bass.ds(e + s, 1), :].squeeze(0).partition_broadcast(P)).then_inc(b_loaded[s], 16)
            for t in range(NT):
                sp.wait_ge(added, (E - 1) * NT + t + 1)
                sp.dma_start(out_v[:, t, :], x1[:, t * D:(t + 1) * D]).then_inc(stored, 16)
            sp.wait_ge(stored, 16 * NT)

        @block.scalar
        def _(act):
            act.sem_inc(z_free, 2)

            def split(e, s):
                act.wait_ge(w_loaded[s], e * 8 + 16)
                act.wait_ge(w_free, e + s + 1)
                nc.scalar.activation(w_hi[:, s, :, :], w_raw[:, s, :, :], ACT.Copy).then_inc(w_hi_done, 1)

            with act.Fori(0, E // 2) as pair:
                e = pair * 2
                for s in range(2):
                    split(e, s)
                for s in range(2):
                    for t in range(NT):
                        n = e * NT + s * NT + t + 1
                        act.wait_ge(z_done, n)
                        act.wait_ge(r_free, n)
                        nc.scalar.activation(r[:, t % 2, :], z[:, t % 2, :], ACT.Relu,
                                             scale=weight[:, bass.ds(e + (t * E + s), 1)]).then_inc(r_done, 1)
                        act.wait_ge(r_done, n)
                        act.sem_inc(z_free, 1)

        @block.vector
        def _(dve):
            dve.sem_inc(w_raw_free, 2)
            dve.sem_inc(b_free, 2)
            dve.sem_inc(r_free, 2)
            dve.sem_inc(y_free, NT)
            with dve.Fori(0, E // 2) as pair:
                e = pair * 2
                for s in range(2):
                    dve.wait_ge(w_hi_done, e + s + 1)
                    nc.vector.tensor_tensor(w_lo[:, s, :, :], w_raw[:, s, :, :], w_hi[:, s, :, :], ALU.subtract).then_inc(w_split, 1)
                    dve.wait_ge(w_split, e + s + 1)
                    dve.sem_inc(w_raw_free, 1)

                def add_bias(s, t):
                    n = e * NT + s * NT + t + 1
                    if t == 0:
                        dve.wait_ge(b_loaded[s], e * 8 + 16)
                    dve.wait_ge(y_done, n)
                    dve.wait_ge(z_free, n)
                    nc.vector.tensor_tensor(z[:, t % 2, :], y_ps[:, t, :], b_bc[:, s, :], ALU.add).then_inc(z_done, 1)

                def accumulate(s, t):
                    n = e * NT + s * NT + t + 1
                    dve.wait_ge(r_done, n)
                    tile = x1[:, t * D:(t + 1) * D]
                    nc.vector.tensor_tensor(tile, tile, r[:, t % 2, :], ALU.add).then_inc(added, 1)
                    dve.wait_ge(added, n)
                    dve.sem_inc(r_free, 1)
                    dve.sem_inc(y_free, 1)

                for s in range(2):
                    for t in range(NT + 1):
                        if t < NT:
                            add_bias(s, t)
                        if t > 0:
                            accumulate(s, t - 1)
                    dve.sem_inc(b_free, 1)

        @block.tensor
        def _(pe):
            pe.sem_inc(w_free, 2)
            with pe.Fori(0, E // 2) as pair:
                e = pair * 2
                for s in range(2):
                    pe.wait_ge(w_split, e + s + 1)
                    for t in range(NT):
                        n = e * NT + s * NT + t + 1
                        tok = slice(t * P, (t + 1) * P)
                        pe.wait_ge(y_free, n)
                        split_product(nc, y_ps[:, t, :], [(x2_hi[:, c, tok], x2_lo[:, c, tok], w_hi[:, s, c, :], w_lo[:, s, c, :])
                                                          for c in range(NC)]).then_inc(y_done, 1)
                pe.wait_ge(y_done, e * NT + 2 * NT)
                pe.sem_inc(w_free, 2)


TOP_K = 2
HEADS, GROUPS, HEAD_DIM = 16, 4, 96


def cross_attention_and_experts(nc, x, ctx_t, wq, wk, wv, wo, wg, bg, we, be, ident, earlier, out, queries):
    T, D = x.shape
    B = ctx_t.shape[0]
    G = HEADS // GROUPS
    xt_dram = nc.dram_tensor("normed_latents_t", (D, T), F32).ap()
    q_dram = nc.dram_tensor("queries_t", (HEADS * HEAD_DIM, T), F32).ap()
    l_dram = nc.dram_tensor("softmax_sums", (GROUPS, G * queries), F32).ap()
    o_dram = nc.dram_tensor("attended_t", (HEADS * HEAD_DIM, T), F32).ap()
    latent_norm_and_queries(nc, x, wq, ident, xt_dram, q_dram)
    attention(nc, ctx_t, wk, wv, ident, xt_dram, q_dram, l_dram, o_dram, B, GROUPS, HEAD_DIM, G, queries)
    NT, NC, E = T // P, D // P, wg.shape[1]
    with (
        nc.sbuf_tensor("x1", [P, NT * D], F32) as x1,
        nc.sbuf_tensor("x2_hi", [P, NC, T], F32R) as x2_hi,
        nc.sbuf_tensor("x2_lo", [P, NC, T], F32R) as x2_lo,
        nc.sbuf_tensor("weight", [P, NT * E], F32) as weight,
    ):
        output_and_router(nc, x, wo, wg, bg, earlier, ident, o_dram, x1, x2_hi, x2_lo, weight)
        experts(nc, we, be, out, x1, x2_hi, x2_lo, weight)


def kernel(x, ctx_4096, L0_xattn_Wq, L0_xattn_Wk, L0_xattn_Wv, L0_xattn_Wo, L0_ffn_W_gate, L0_ffn_b_gate,
           L0_ffn_W_e, L0_ffn_b_e):
    import numpy as np
    import concourse.bacc as bacc
    from concourse.bass_utils import run_bass_kernel_spmd

    B, Q, D = x.shape
    E = L0_ffn_W_gate.shape[1]
    arrays = {
        "x": np.reshape(x, (B * Q, D)),
        "context_t": np.transpose(ctx_4096, (0, 2, 1)),
        "wq_t": np.transpose(L0_xattn_Wq),
        "wk_t": np.transpose(L0_xattn_Wk),
        "wv_t": np.transpose(L0_xattn_Wv),
        "wo_t": np.transpose(L0_xattn_Wo),
        "w_gate": L0_ffn_W_gate,
        "b_gate": L0_ffn_b_gate,
        "w_e": L0_ffn_W_e,
        "b_e": L0_ffn_b_e,
        "identity": np.eye(P, dtype=np.float32),
        "earlier": np.broadcast_to(np.tril(np.ones((E, E), np.float32), -1).reshape(1, E * E), (P, E * E)),
    }
    arrays = {name: np.ascontiguousarray(a) for name, a in arrays.items()}
    nc = bacc.Bacc("TRN2", target_bir_lowering=False, num_devices=1)
    args = [nc.dram_tensor(name, a.shape, mybir.dt.from_np(a.dtype), kind="ExternalInput").ap()
            for name, a in arrays.items()]
    out = nc.dram_tensor("out", (B * Q, D), F32, kind="ExternalOutput").ap()
    cross_attention_and_experts(nc, *args, out, Q)
    result = run_bass_kernel_spmd(nc, [arrays], core_ids=[0])
    return np.reshape(result.results[0]["out"], (B, Q, D))
```

```python
from contextlib import ExitStack

import concourse.bass as bass
from concourse import mybir

F32 = mybir.dt.float32
F32R = mybir.dt.float32r
ALU = mybir.AluOpType
ACT = mybir.ActivationFunctionType
AX_X = mybir.AxisListType.X

P = 128
BANK = 512
EPS = 1e-5


def three_passes(w_hi, w_lo, m_hi, m_lo):
    return ((w_hi, m_hi), (w_hi, m_lo), (w_lo, m_hi))


def split_product(nc, out, blocks, between=()):
    between = list(between)
    total = len(between)
    pairs = [pair for block in blocks for pair in three_passes(*block)]
    for n, (stationary, moving) in enumerate(pairs):
        last = nc.tensor.matmul(out, stationary, moving, start=(n == 0), stop=(n == len(pairs) - 1))
        while between and n + 1 >= len(pairs) * (total - len(between) + 1) // (total + 1):
            between.pop(0)()
    return last


def key_rows(kvd):
    hd = kvd // GROUPS
    tail = P - hd
    assert (GROUPS - 1) * tail == hd and (GROUPS - 1) * P == kvd and hd % 32 == 0 and tail == 32
    return hd, tail


def latent_norm_and_queries(nc, x, wq, wk, wv, ident_in, xt_dram, q_dram, wkv, ident, landing):
    T, D = x.shape
    QD, KVD = wq.shape[1], wk.shape[1]
    NT, NC, NM = T // P, D // P, QD // P
    HALVES = T // BANK
    WCOLS = landing.shape[3]
    NQW = QD // WCOLS
    BLOCKS = WCOLS // P
    NB = 4
    x_v = x.rearrange("(t p) d -> p t d", p=P)
    wq_v = wq.rearrange("(c p) m -> p c m", p=P)
    wk_v = wk.rearrange("(c p) m -> p c m", p=P)
    wv_v = wv.rearrange("(c p) m -> p c m", p=P)
    xt_v = xt_dram.rearrange("(c p) t -> p c t", p=P)
    HD, TAIL = key_rows(KVD)

    with ExitStack() as ctx:
        def sb(name, shape, dt=F32):
            return ctx.enter_context(nc.sbuf_tensor(name, shape, dt))

        def sem(name):
            return ctx.enter_context(nc.semaphore(name))

        x_sb = sb("n1_x", [P, NT, D])
        stats = sb("n1_stats", [P, NT, 6])
        mean_var = sb("n1_mean_var", [P, NT, 2])
        var_eps = sb("n1_var_eps", [P, NT])
        std = sb("n1_std", [P, NT])
        rstd = sb("n1_rstd", [P, NT])
        xn = sb("n1_xn", [P, 2, D])
        xt_hi = sb("n1_xt_hi", [P, NC, T], F32R)
        xt_lo = sb("n1_xt_lo", [P, NC, T], F32R)
        xt_raw = sb("n1_xt_raw", [P, 2, NC, P])
        wq_hi = sb("q_w_hi", [P, NQW, NC, WCOLS], F32R)
        wq_lo = sb("q_w_lo", [P, NQW, NC, WCOLS], F32R)
        q_sb = sb("q_sb", [P, NB, BANK])
        xt_ps = ctx.enter_context(nc.psum_tensor("n1_xt_ps", [P, 2, NC, P], F32))
        q_ps = ctx.enter_context(nc.psum_tensor("q_ps", [P, NB, BANK], F32))
        wk_hi, wk_lo, wv_hi, wv_lo = wkv
        parts_hi = [wq_hi[:, n, :, :] for n in range(NQW)] + [wk_hi[:], wv_hi[:]]
        parts_lo = [wq_lo[:, n, :, :] for n in range(NQW)] + [wk_lo[:], wv_lo[:]]
        NW = len(parts_hi)

        x_loaded = [sem(f"n1_x_loaded{t}") for t in range(NT)]
        ident_loaded = sem("n1_ident_loaded")
        stats_done = sem("n1_stats_done")
        mean_var_done = sem("n1_mean_var_done")
        var_eps_done = sem("n1_var_eps_done")
        std_done = sem("n1_std_done")
        rstd_done = sem("n1_rstd_done")
        xn_done = sem("n1_xn_done")
        xt_done = sem("n1_xt_done")
        xt_raw_done = sem("n1_xt_raw_done")
        xt_split = sem("n1_xt_split")
        xt_stored = [sem(f"n1_xt_stored{s}") for s in range(2)]
        w_loaded = [sem(f"q_w_loaded{s}") for s in range(2)]
        w_hi_done = sem("q_w_hi_done")
        w_split = sem("q_w_split")
        q_done = sem("q_done")
        q_copied = sem("q_copied")
        q_stored = [sem(f"q_stored{n}") for n in range(NB)]

        block = ctx.enter_context(nc.Block())
        groups = [(m, half) for m in range(NM) for half in range(HALVES)]

        @block.sync
        def _(sp):
            for t in range(NT):
                sp.dma_start(x_sb[:, t, :], x_v[:, t, :]).then_inc(x_loaded[t], 16)
                if t == 0:
                    sp.dma_start(ident[:], ident_in).then_inc(ident_loaded, 16)
                if t < 2:
                    sp.dma_start(landing[:, t, :, :], wq_v[:, :, t * WCOLS:(t + 1) * WCOLS]).then_inc(w_loaded[t], 16)
            for n in range(2, NW):
                sp.wait_ge(w_split, n - 1)
                dst = landing[:, n % 2, :, :]
                if n < NQW:
                    sp.dma_start(dst, wq_v[:, :, n * WCOLS:(n + 1) * WCOLS]).then_inc(w_loaded[n % 2], 16)
                elif n == NQW:
                    for m in range(BLOCKS):
                        sp.dma_start(dst[:, :, m * P:m * P + HD], wk_v[:, :, m * HD:(m + 1) * HD]).then_inc(w_loaded[n % 2], 16)
                        sp.dma_start(dst[:, :, m * P + HD:(m + 1) * P],
                                     wk_v[:, :, BLOCKS * HD + m * TAIL:BLOCKS * HD + (m + 1) * TAIL]).then_inc(w_loaded[n % 2], 16)
                else:
                    sp.dma_start(dst, wv_v).then_inc(w_loaded[n % 2], 16)

        @block.gpsimd
        def _(pool):
            for t in range(NT):
                pool.wait_ge(xt_raw_done, t + 1)
                pool.dma_start(xt_v[:, :, t * P:(t + 1) * P], xt_raw[:, t % 2, :, :]).then_inc(xt_stored[t % 2], 16)
            for n, (m, half) in enumerate(groups):
                pool.wait_ge(q_copied, n + 1)
                pool.dma_start(q_dram[m * P:(m + 1) * P, half * BANK:(half + 1) * BANK], q_sb[:, n % NB, :]).then_inc(q_stored[n % NB], 16)
            for n in range(NB):
                pool.wait_ge(q_stored[n], 16 * len(groups) // NB)
            for s in range(2):
                pool.wait_ge(xt_stored[s], 16 * NT // 2)

        def w_loads(n):
            return 16 * sum(2 * BLOCKS if i == NQW else 1 for i in range(n % 2, n + 1, 2))

        @block.vector
        def _(dve):
            for t in range(NT):
                dve.wait_ge(x_loaded[t], 16)
                nc.vector.bn_stats(stats[:, t, :], x_sb[:, t, :]).then_inc(stats_done, 1)
            for t in range(NT):
                dve.wait_ge(stats_done, t + 1)
                nc.vector.bn_aggr(mean_var[:, t, :], stats[:, t, :]).then_inc(mean_var_done, 1)
            dve.wait_ge(mean_var_done, NT)
            nc.vector.tensor_scalar_add(var_eps[:], mean_var[:, :, 1], EPS).then_inc(var_eps_done, 1)
            dve.wait_ge(std_done, 1)
            nc.vector.reciprocal(rstd[:], std[:]).then_inc(rstd_done, 1)
            dve.wait_ge(rstd_done, 1)

            def split(t):
                dve.wait_ge(xt_raw_done, t + 1)
                nc.vector.tensor_tensor(xt_lo[:, :, t * P:(t + 1) * P], xt_ps[:, t % 2, :, :],
                                        xt_hi[:, :, t * P:(t + 1) * P], ALU.subtract).then_inc(xt_split, 1)

            def split_w(n):
                dve.wait_ge(w_hi_done, n + 1)
                nc.vector.tensor_tensor(parts_lo[n], landing[:, n % 2, :, :], parts_hi[n], ALU.subtract).then_inc(w_split, 1)

            for t in range(NT):
                if t >= 2:
                    dve.wait_ge(xt_done, t - 1)
                nc.vector.tensor_scalar(xn[:, t % 2, :], x_sb[:, t, :], mean_var[:, t, 0:1], rstd[:, t:t + 1],
                                        ALU.subtract, ALU.mult).then_inc(xn_done, 1)
                if t == 0:
                    split_w(0)
                if t >= 1:
                    split(t - 1)
            split(NT - 1)
            for n in range(1, NW):
                split_w(n)

        @block.scalar
        def _(act):
            def round_w(n):
                act.wait_ge(w_loaded[n % 2], w_loads(n))
                nc.scalar.activation(parts_hi[n], landing[:, n % 2, :, :], ACT.Copy).then_inc(w_hi_done, 1)

            def copy_q(n):
                act.wait_ge(q_done, n + 1)
                if n >= NB:
                    act.wait_ge(q_stored[n % NB], 16 * (n // NB))
                nc.scalar.activation(q_sb[:, n % NB, :], q_ps[:, n % NB, :], ACT.Copy).then_inc(q_copied, 1)

            round_w(0)
            act.wait_ge(var_eps_done, 1)
            nc.scalar.activation(std[:], var_eps[:], ACT.Sqrt).then_inc(std_done, 1)
            for t in range(NT):
                act.wait_ge(xt_done, t + 1)
                nc.scalar.activation(xt_hi[:, :, t * P:(t + 1) * P], xt_ps[:, t % 2, :, :], ACT.Copy)
                if t >= 2:
                    act.wait_ge(xt_stored[t % 2], 16 * (t // 2))
                nc.scalar.activation(xt_raw[:, t % 2, :, :], xt_ps[:, t % 2, :, :], ACT.Copy).then_inc(xt_raw_done, 1)
            per = BLOCKS * HALVES
            round_w(1)
            for n in range(len(groups)):
                if n % per == 1 and n // per + 2 < NW:
                    round_w(n // per + 2)
                copy_q(n)

        @block.tensor
        def _(pe):
            pe.wait_ge(ident_loaded, 16)
            for t in range(NT):
                pe.wait_ge(xn_done, t + 1)
                if t >= 2:
                    pe.wait_ge(xt_split, t - 1)
                for c in range(NC):
                    last = nc.tensor.transpose(xt_ps[:, t % 2, c, :], xn[:, t % 2, c * P:(c + 1) * P], ident[:])
                last.then_inc(xt_done, 1)
            pe.wait_ge(xt_split, NT)
            for n, (m, half) in enumerate(groups):
                part, i = divmod(m, BLOCKS)
                if i == 0 and half == 0:
                    pe.wait_ge(w_split, part + 1)
                if n >= NB:
                    pe.wait_ge(q_copied, n - NB + 1)
                rows, cols = slice(i * P, (i + 1) * P), slice(half * BANK, (half + 1) * BANK)
                split_product(nc, q_ps[:, n % NB, :],
                              [(wq_hi[:, part, c, rows], wq_lo[:, part, c, rows], xt_hi[:, c, cols], xt_lo[:, c, cols])
                               for c in range(NC)]).then_inc(q_done, 1)


def attention(nc, ctx_t, wkv, ident, h_raw, xt_dram, q_dram, l_dram, o_dram, B, KV, HD, G, Q):
    CTX = ctx_t.shape[2]
    D = ctx_t.shape[1]
    NC = D // P
    S = CTX + Q
    CW = 3 * P
    CHUNKS = [(s0, min(CW, S - s0)) for s0 in range(0, S, CW)]
    TILES = [(s0, min(P, S - s0)) for s0 in range(0, S, P)]
    NCH, NTL = len(CHUNKS), len(TILES)
    SE = S + S % 2
    GQ = G * Q
    NJ = GQ // P
    QS = G * HD
    R = HD + 1
    SCALE = float(HD) ** -0.5
    KVD = KV * HD
    HV = GQ // BANK
    NG = KV * NTL
    BLOCKS = KVD // P
    TAIL = P - HD
    PC = BLOCKS + CW // P
    NPR = PC * NCH
    NJB = NJ * NCH
    JOBS_AT, JOBS_PER = 2, 4
    M_AT = JOBS_AT + NJB // JOBS_PER
    INVERT_AT, NORM_AT = 5, 9
    ONE = 1
    assert KVD == CW and GQ == 2 * BANK and NG % 6 == 0 and NJB % 2 == 0 and M_AT < NTL - 1

    wk_hi, wk_lo, wv_hi, wv_lo = wkv
    ctx_v = ctx_t.rearrange("b (c p) s -> p (b c) s", p=P)
    xt_v = xt_dram.rearrange("(c p) t -> p c t", p=P)
    q_v = q_dram.rearrange("(h d) t -> d h t", d=HD)
    o_v = o_dram.rearrange("(h d) t -> d h t", d=HD)

    with ExitStack() as ctx:
        def sb(name, shape, dt=F32):
            return ctx.enter_context(nc.sbuf_tensor(name, shape, dt))

        def pb(name, shape):
            return ctx.enter_context(nc.psum_tensor(name, shape, F32))

        def sem(name):
            return ctx.enter_context(nc.semaphore(name))

        kt_hi = sb("a_kt_hi", [R, KV, SE], F32R)
        kt_lo = sb("a_kt_lo", [R, KV, SE], F32R)
        v_hi = sb("a_v_hi", [P, NTL, KV, R], F32R)
        v_lo = sb("a_v_lo", [P, NTL, KV, R], F32R)
        work = sb("a_work", [P, 2, 3 * GQ], F32R)
        q_raw = sb("a_q_raw", [HD, G, Q])
        q_hi = sb("a_q_hi", [R, 2, GQ], F32R)
        q_lo = sb("a_q_lo", [HD, 2, GQ], F32R)
        o_sb = sb("a_o_sb", [R, GQ])
        l_rows = sb("a_l_rows", [NJ, P])
        l_inv = sb("a_l_inv", [NJ, P])
        l_bc = sb("a_l_bc", [HD, GQ])
        m_part = sb("a_m_part", [P, NJ, NCH])
        m_all = sb("a_m_all", [P, NJ])
        m_row = sb("a_m_row", [NJ, P], F32R)
        s_ps = pb("a_s_ps", [P, 2, HV, BANK])
        o_ps = pb("a_o_ps", [P, HV, BANK])
        m_ps = pb("a_m_ps", [P, 2, BANK])
        pr_ps = [s_ps[:, n // 2, n % 2, :] for n in range(4)]

        def h_at(part, c):
            return work[:, part, c % 2 * NC * CW:(c % 2 + 1) * NC * CW].rearrange("p (c s) -> p c s", c=NC)

        def p_at(part, g):
            return work[:, part, g % 3 * GQ:(g % 3 + 1) * GQ]

        ones_set = sem("a_ones_set")
        h_loaded = [sem(f"a_h_loaded{s}") for s in range(2)]
        h_hi_done = sem("a_h_hi_done")
        h_split = sem("a_h_split")
        pr_done = sem("a_pr_done")
        pr_hi_done = sem("a_pr_hi_done")
        pr_split = sem("a_pr_split")
        q_loaded = sem("a_q_loaded")
        q_hi_done = sem("a_q_hi_done")
        q_split = sem("a_q_split")
        mm_done = sem("a_mm_done")
        mm_reduced = sem("a_mm_reduced")
        m_all_done = sem("a_m_all_done")
        m_turned = sem("a_m_turned")
        m_row_done = sem("a_m_row_done")
        m_row_placed = sem("a_m_row_placed")
        s_done = sem("a_s_done")
        exp_done = sem("a_exp_done")
        p_split = sem("a_p_split")
        pv_done = sem("a_pv_done")
        o_copied = sem("a_o_copied")
        l_moved = sem("a_l_moved")
        l_stored = sem("a_l_stored")
        l_spread = sem("a_l_spread")
        l_inverted = sem("a_l_inverted")
        o_normed = sem("a_o_normed")
        o_stored = sem("a_o_stored")
        o_sb_free = sem("a_o_sb_free")

        def jobs_of(g):
            kv, t = divmod(g, NTL)
            if kv + 1 >= KV or not JOBS_AT <= t < M_AT:
                return []
            n0 = (t - JOBS_AT) * JOBS_PER
            return [(kv + 1, n) for n in range(n0, n0 + JOBS_PER)]

        def projections(c):
            ks = [("k", PC * c + m, m) for m in range(BLOCKS)]
            vs = [("v", PC * c + BLOCKS + i, 3 * c + i) for i in range(CW // P)]
            counts = (0, 0, 2, 2, 2, 2) if c < NCH - 1 else (0, 4, 4, 0, 0, 0)
            assert sum(counts) == NJ
            n = c * NJ
            for item, count in zip(ks + vs, counts):
                yield (*item, list(range(n, n + count)))
                n += count

        def key_pieces(m):
            return ((m, slice(0, HD), slice(0, HD)), (KV - 1, slice(HD, P), slice(m * TAIL, (m + 1) * TAIL)))

        def even(w):
            return w + w % 2

        block = ctx.enter_context(nc.Block())

        @block.gpsimd
        def _(pool):
            with pool.Fori(0, B) as b:
                def load_q(kv):
                    pool.wait_ge(q_split, ONE + b * KV + kv)
                    pool.dma_start(q_raw[:], q_v[:, kv * G:(kv + 1) * G, bass.ds(b * Q, Q)]).then_inc(q_loaded, 16)

                load_q(0)
                for c, (s0, w) in enumerate(CHUNKS):
                    pool.wait_ge(h_split, ONE + b * NCH + (c - 1 if c >= 2 else 0))
                    wc = min(w, CTX - s0)
                    pool.dma_start(h_raw[:, c % 2, :, 0:wc], ctx_v[:, bass.ds(b * NC, NC), s0:s0 + wc]).then_inc(h_loaded[c % 2], 16)
                    if wc < w:
                        pool.dma_start(h_raw[:, c % 2, :, wc:w], xt_v[:, :, bass.ds(b * Q, Q)]).then_inc(h_loaded[c % 2], 16)
                for kv in range(1, KV):
                    load_q(kv)

        @block.sync
        def _(sp):
            sp.sem_inc(o_sb_free, ONE)
            with sp.Fori(0, B) as b:
                def place_m(kv):
                    sp.wait_ge(m_row_done, b * KV + kv + 1)
                    sp.dma_start(q_hi[HD:R, kv % 2, :].bitcast(F32).rearrange("o (j t) -> o j t", j=NJ),
                                 m_row[:].bitcast(F32)).then_inc(m_row_placed, 16)

                def spread_sums(kv):
                    n = b * KV + kv + 1
                    sp.wait_ge(o_copied, ONE + n)
                    sp.dma_start(l_rows[:], o_sb[HD:R, :].rearrange("o (j t) -> o j t", j=NJ)).then_inc(l_moved, 16)
                    sp.wait_ge(l_inverted, n)
                    sp.dma_start(l_dram.rearrange("(j t) -> j t", j=NJ), l_inv[:]).then_inc(l_stored, 16)
                    sp.wait_ge(l_stored, n * 16)
                    sp.dma_start(l_bc[:], l_dram.partition_broadcast(HD)).then_inc(l_spread, 16)
                    sp.wait_ge(o_normed, n)
                    sp.dma_start(o_v[:, kv * G:(kv + 1) * G, bass.ds(b * Q, Q)],
                                 o_sb[0:HD, :].rearrange("d (g q) -> d g q", g=G)).then_inc(o_stored, 16)
                    sp.wait_ge(o_stored, n * 16)
                    sp.sem_inc(o_sb_free, 1)

                place_m(0)
                place_m(1)
                for kv in range(KV):
                    spread_sums(kv)
                    if kv + 2 < KV:
                        place_m(kv + 2)

        @block.scalar
        def _(act):
            act.sem_inc(o_copied, ONE)

            def split_q(b, kv):
                act.wait_ge(q_loaded, (b * KV + kv + 1) * 16)
                nc.scalar.activation(q_hi[0:HD, kv % 2, :], q_raw[:].rearrange("d g q -> d (g q)"),
                                     ACT.Copy).then_inc(q_hi_done, 1)

            def split_h(b, c):
                if c >= 2:
                    act.wait_ge(pr_done, b * NPR + PC * (c - 1))
                per = (64, 32)[c % 2]
                act.wait_ge(h_loaded[c % 2], b * per + (16 * (c // 2 + 1) if c < NCH - 1 else per))
                w = even(CHUNKS[c][1])
                nc.scalar.activation(h_at(0, c)[:, :, 0:w], h_raw[:, c % 2, :, 0:w], ACT.Copy).then_inc(h_hi_done, 1)

            def copy_o(b, kv):
                act.wait_ge(pv_done, ONE + b * NG + (kv + 1) * NTL)
                act.wait_ge(o_sb_free, ONE + b * KV + kv)
                nc.scalar.activation(o_sb[:], o_ps[0:R, :, :].rearrange("p a n -> p (a n)"), ACT.Copy).then_inc(o_copied, 1)

            def project(b, before):
                act.wait_ge(pv_done, ONE + b * NG)
                split_h(b, 0)
                split_q(b, 0)
                split_h(b, 1)
                if before is not None:
                    copy_o(before, KV - 1)
                for c, (s0, w) in enumerate(CHUNKS):
                    w = even(w)
                    for what, n, i, _jobs in projections(c):
                        act.wait_ge(pr_done, b * NPR + n + 1)
                        if what == "k":
                            for kv, src, dst in key_pieces(i):
                                last = nc.scalar.activation(kt_hi[dst, kv, s0:s0 + w], pr_ps[n % 4][src, 0:w], ACT.Copy)
                        else:
                            m = TILES[i][1]
                            last = nc.scalar.activation(v_hi[0:m, i, :, 0:HD],
                                                        pr_ps[n % 4][0:m, 0:KVD].rearrange("p (k d) -> p k d", k=KV), ACT.Copy)
                        last.then_inc(pr_hi_done, 1)
                    if c + 2 < NCH:
                        split_h(b, c + 2)

            def attend(b):
                for g in range(NG):
                    kv, t = divmod(g, NTL)
                    m = TILES[t][1]
                    act.wait_ge(s_done, b * NG + g + 1)
                    if g >= 3:
                        act.wait_ge(pv_done, ONE + b * NG + g - 2)
                    s_in = s_ps[0:m, g % 2, :, :].rearrange("p a n -> p (a n)")
                    nc.scalar.activation(p_at(0, g)[0:m, :], s_in, ACT.Exp, scale=SCALE)
                    nc.scalar.activation(s_in, s_in, ACT.Exp, scale=SCALE).then_inc(exp_done, 1)
                    if t == 0 and kv + 1 < KV:
                        split_q(b, kv + 1)
                    if t == 1 and kv > 0:
                        copy_o(b, kv - 1)

            project(0, None)
            with act.Fori(0, B - 1) as b:
                attend(b)
                project(b + 1, b)
            attend(B - 1)
            copy_o(B - 1, KV - 1)

        @block.vector
        def _(dve):
            nc.vector.memset(kt_hi[HD:R, :, :].bitcast(F32), 1.0).then_inc(ones_set, 1)
            nc.vector.memset(v_hi[:, :, :, HD:R].bitcast(F32), 1.0).then_inc(ones_set, 1)
            nc.vector.memset(v_lo[:, :, :, HD:R].bitcast(F32), 0.0).then_inc(ones_set, 1)
            dve.sem_inc(q_split, ONE)
            dve.sem_inc(h_split, ONE)
            dve.sem_inc(mm_reduced, ONE)

            def split_q(b, kv):
                dve.wait_ge(q_hi_done, b * KV + kv + 1)
                nc.vector.tensor_tensor(q_lo[:, kv % 2, :], q_raw[:].rearrange("d g q -> d (g q)"),
                                        q_hi[0:HD, kv % 2, :], ALU.subtract).then_inc(q_split, 1)

            def split_h(b, c):
                dve.wait_ge(h_hi_done, b * NCH + c + 1)
                w = even(CHUNKS[c][1])
                nc.vector.tensor_tensor(h_at(1, c)[:, :, 0:w], h_raw[:, c % 2, :, 0:w], h_at(0, c)[:, :, 0:w],
                                        ALU.subtract).then_inc(h_split, 1)

            def reduce_job(b, kv, n):
                c, j = divmod(n, NJ)
                dve.wait_ge(mm_done, b * KV * NJB + kv * NJB + n + 1)
                nc.vector.reduce_max(m_part[:, j, c:c + 1], m_ps[:, n % 2, 0:CHUNKS[c][1]], AX_X).then_inc(mm_reduced, 1)

            def join_m(b, kv):
                dve.wait_ge(mm_reduced, ONE + b * KV * NJB + (kv + 1) * NJB)
                nc.vector.reduce_max(m_all[:], m_part[:], AX_X).then_inc(m_all_done, 1)

            def finish_m(b, kv):
                dve.wait_ge(m_turned, b * KV + kv + 1)
                nc.vector.tensor_scalar(m_row[:], m_ps[0:NJ, 0, 0:P], -1.0, None, ALU.mult).then_inc(m_row_done, 1)

            def split_p(b, g):
                m = TILES[g % NTL][1]
                dve.wait_ge(exp_done, b * NG + g + 1)
                nc.vector.tensor_tensor(p_at(1, g)[0:m, :], s_ps[0:m, g % 2, :, :].rearrange("p a n -> p (a n)"),
                                        p_at(0, g)[0:m, :], ALU.subtract).then_inc(p_split, 1)

            def invert_sums(b, kv):
                dve.wait_ge(l_moved, (b * KV + kv + 1) * 16)
                nc.vector.reciprocal(l_inv[:], l_rows[:]).then_inc(l_inverted, 1)

            def norm(b, kv):
                dve.wait_ge(l_spread, (b * KV + kv + 1) * 16)
                nc.vector.tensor_tensor(o_sb[0:HD, :], o_sb[0:HD, :], l_bc[:], ALU.mult).then_inc(o_normed, 1)

            def project(b, before):
                split_h(b, 0)
                split_q(b, 0)
                split_h(b, 1)
                for c, (s0, w) in enumerate(CHUNKS):
                    w = even(w)
                    for what, n, i, jobs in projections(c):
                        for job in jobs:
                            reduce_job(b, 0, job)
                        if c == NCH - 1 and what == "v" and i == NTL - 3:
                            join_m(b, 0)
                        if c == NCH - 1 and what == "v" and i == NTL - 2:
                            finish_m(b, 0)
                        dve.wait_ge(pr_hi_done, b * NPR + n + 1)
                        if what == "k":
                            for kv, src, dst in key_pieces(i):
                                last = nc.vector.tensor_tensor(kt_lo[dst, kv, s0:s0 + w], pr_ps[n % 4][src, 0:w],
                                                               kt_hi[dst, kv, s0:s0 + w], ALU.subtract)
                        else:
                            m = TILES[i][1]
                            last = nc.vector.tensor_tensor(v_lo[0:m, i, :, 0:HD],
                                                           pr_ps[n % 4][0:m, 0:KVD].rearrange("p (k d) -> p k d", k=KV),
                                                           v_hi[0:m, i, :, 0:HD], ALU.subtract)
                        last.then_inc(pr_split, 1)
                    if c + 2 < NCH:
                        split_h(b, c + 2)
                    if before is not None and c == 0:
                        invert_sums(before, KV - 1)
                    if before is not None and c == 1:
                        norm(before, KV - 1)

            def attend(b):
                for g in range(NG + 1):
                    kv, t = divmod(g, NTL)
                    if g >= 1:
                        split_p(b, g - 1)
                    if t == 1 and kv + 1 < KV:
                        split_q(b, kv + 1)
                    if t == INVERT_AT and kv > 0:
                        invert_sums(b, kv - 1)
                    if t == NORM_AT and kv > 0:
                        norm(b, kv - 1)
                    for job in jobs_of(g):
                        reduce_job(b, *job)
                    if t == M_AT and kv + 1 < KV:
                        join_m(b, kv + 1)
                        finish_m(b, kv + 1)

            project(0, None)
            with dve.Fori(0, B - 1) as b:
                attend(b)
                project(b + 1, b)
            attend(B - 1)
            invert_sums(B - 1, KV - 1)
            norm(B - 1, KV - 1)

        @block.tensor
        def _(pe):
            pe.wait_ge(ones_set, 3)
            pe.sem_inc(pv_done, ONE)

            def job(b, kv, n):
                c, j = divmod(n, NJ)
                s0, w = CHUNKS[c]
                w = even(w)
                if kv > 0 or n >= 2:
                    pe.wait_ge(mm_reduced, ONE + b * KV * NJB + kv * NJB + n - 1)
                nc.tensor.matmul(m_ps[:, n % 2, 0:w], q_hi[0:HD, kv % 2, j * P:(j + 1) * P], kt_hi[0:HD, kv, s0:s0 + w],
                                 start=True, stop=True).then_inc(mm_done, 1)

            def first_job(b, n):
                if n % NJ == 0:
                    pe.wait_ge(q_split, ONE + b * KV + 1)
                    pe.wait_ge(pr_split, b * NPR + n // NJ * PC + 1)
                job(b, 0, n)

            def turn_m(b, kv):
                pe.wait_ge(m_all_done, b * KV + kv + 1)
                nc.tensor.transpose(m_ps[0:NJ, 0, 0:P], m_all[:], ident[:]).then_inc(m_turned, 1)

            def scores(g, half):
                kv, t = divmod(g, NTL)
                s0, m = TILES[t]
                keys = slice(s0, s0 + m)
                cols = slice(half * BANK, (half + 1) * BANK)
                out = s_ps[0:m, g % 2, half, :]
                nc.tensor.matmul(out, kt_hi[0:R, kv, keys], q_hi[0:R, kv % 2, cols], start=True, stop=False)
                nc.tensor.matmul(out, kt_hi[0:HD, kv, keys], q_lo[0:HD, kv % 2, cols], start=False, stop=False)
                return nc.tensor.matmul(out, kt_lo[0:HD, kv, keys], q_hi[0:HD, kv % 2, cols], start=False, stop=True)

            def values(g, half):
                kv, t = divmod(g, NTL)
                m = TILES[t][1]
                cols = slice(half * BANK, (half + 1) * BANK)
                pairs = three_passes(v_hi[0:m, t, kv, :], v_lo[0:m, t, kv, :], p_at(0, g)[0:m, cols], p_at(1, g)[0:m, cols])
                for n, (stationary, moving) in enumerate(pairs):
                    last = nc.tensor.matmul(o_ps[0:R, half, :], stationary, moving,
                                            start=(t == 0 and n == 0), stop=(t == NTL - 1 and n == 2))
                return last

            def project(b):
                for c, (s0, w) in enumerate(CHUNKS):
                    w = even(w)
                    pe.wait_ge(h_split, ONE + b * NCH + c + 1)
                    h_hi, h_lo = h_at(0, c), h_at(1, c)
                    for what, n, i, jobs in projections(c):
                        if n >= 4:
                            pe.wait_ge(pr_split, b * NPR + n - 3)
                        between = [lambda job=job: first_job(b, job) for job in jobs]
                        if what == "k":
                            rows = slice(i * P, (i + 1) * P)
                            last = split_product(nc, pr_ps[n % 4][:, 0:w],
                                                 [(wk_hi[:, k, rows], wk_lo[:, k, rows], h_hi[:, k, 0:w], h_lo[:, k, 0:w])
                                                  for k in range(NC)], between)
                        else:
                            m = TILES[i][1]
                            at = i % (CW // P) * P
                            last = split_product(nc, pr_ps[n % 4][0:m, 0:KVD],
                                                 [(h_hi[:, k, at:at + m], h_lo[:, k, at:at + m], wv_hi[:, k, :], wv_lo[:, k, :])
                                                  for k in range(NC)], between)
                        last.then_inc(pr_done, 1)
                        if c == NCH - 1 and what == "v" and i == NTL - 3:
                            turn_m(b, 0)

            def attend(b):
                pe.wait_ge(pr_split, (b + 1) * NPR)
                for g in range(NG + 2):
                    kv, t = divmod(g, NTL)
                    jobs = jobs_of(g)
                    if jobs and t == JOBS_AT:
                        pe.wait_ge(q_split, ONE + b * KV + kv + 2)
                    if g < NG:
                        if t == 0:
                            pe.wait_ge(m_row_placed, (b * KV + kv + 1) * 16)
                            pe.wait_ge(q_split, ONE + b * KV + kv + 1)
                        if g >= 2:
                            pe.wait_ge(p_split, b * NG + g - 1)
                        scores(g, 0)
                        if jobs:
                            job(b, *jobs[0])
                        scores(g, 1).then_inc(s_done, 1)
                        if jobs:
                            job(b, *jobs[1])
                        if t == M_AT and kv + 1 < KV:
                            turn_m(b, kv + 1)
                    if g >= 2:
                        if g >= NG:
                            pe.wait_ge(p_split, b * NG + g - 1)
                        if (g - 2) % NTL == 0:
                            pe.wait_ge(o_copied, ONE + b * KV + kv)
                        values(g - 2, 0)
                        if jobs:
                            job(b, *jobs[2])
                        values(g - 2, 1).then_inc(pv_done, 1)
                        if jobs:
                            job(b, *jobs[3])

            project(0)
            with pe.Fori(0, B - 1) as b:
                attend(b)
                project(b + 1)
            attend(B - 1)


def output_router_experts(nc, x, wo, wg, bg, we, be, earlier_in, ident, o_dram, out):
    T, D = x.shape
    QD = wo.shape[0]
    E, _, H = we.shape
    NT, NC, NK = T // P, D // P, QD // P
    PARTS = 4
    KP = NK // PARTS
    E0, T0 = 2 * NT, 2
    x_v = x.rearrange("(t p) d -> t p d", p=P)
    wo_v = wo.rearrange("(k p) d -> p k d", p=P)
    o_v = o_dram.rearrange("(k p) t -> p k t", p=P)
    we_v = we.rearrange("e (c p) h -> p (e c) h", p=P)
    out_v = out.rearrange("(t p) h -> t p h", p=P)
    assert E % 2 == 0 and 2 * NC <= NK and H == D == BANK and NT == 8

    with ExitStack() as ctx:
        def sb(name, shape, dt=F32):
            return ctx.enter_context(nc.sbuf_tensor(name, shape, dt))

        def sem(name):
            return ctx.enter_context(nc.semaphore(name))

        x1 = sb("x1", [P, NT, D])
        x2_hi = sb("x2_hi", [P, NC, T], F32R)
        x2_lo = sb("x2_lo", [P, NC, T], F32R)
        weight = sb("weight", [P, NT * E])
        wg_sb = sb("o_wg", [P, NC, E])
        bg_bc = sb("o_bg", [P, E])
        earlier = sb("o_earlier", [P, E, E])
        wo_raw = sb("o_w_raw", [P, 2, KP, D])
        w_hi = sb("o_w_hi", [P, NK, D], F32R)
        w_lo = sb("o_w_lo", [P, NK, D], F32R)
        o_raw = sb("o_raw", [P, 2, NK, P])
        o_hi = sb("o_hi", [P, 2, NK, P], F32R)
        o_lo = sb("o_lo", [P, 2, NK, P], F32R)
        x_sb = sb("o_x", [P, 2, D])
        stats = sb("o_stats", [P, NT, 6])
        mean_var = sb("o_mean_var", [P, NT, 2])
        var_eps = sb("o_var_eps", [P, NT])
        std = sb("o_std", [P, NT])
        rstd = sb("o_rstd", [P, NT])
        xn = sb("o_xn", [P, 2, D])
        x2_raw = sb("o_x2_raw", [P, 2, NC, P])
        logits = sb("o_logits", [P, NT, E])
        above = sb("o_above", [P, NT, E, E])
        same = sb("o_same", [P, NT, E, E])
        rank = sb("o_rank", [P, NT, E])
        we_raw = sb("e_w_raw", [P, 2, NC, H])
        b_bc = sb("e_b", [P, 2, H])
        z = sb("e_z", [P, 2, H])
        r = sb("e_r", [P, 2, H])
        ps = ctx.enter_context(nc.psum_tensor("e_ps", [P, NT, BANK], F32))
        y_at = [ps[:, n, :] for n in (0, 1)]
        x2_at = [ps[:, n, :].rearrange("p (c t) -> p c t", c=NC) for n in (2, 3)]
        g_at = [ps[:, n, 0:E] for n in (4, 5)]

        wg_loaded = sem("o_wg_loaded")
        const_loaded = sem("o_const_loaded")
        wo_loaded = [sem(f"o_w_loaded{n}") for n in range(2)]
        wo_hi_done = sem("o_w_hi_done")
        wo_split = sem("o_w_split")
        o_loaded = [sem(f"o_loaded{s}") for s in range(2)]
        x_loaded = [sem(f"o_x_loaded{s}") for s in range(2)]
        o_hi_done = sem("o_hi_done")
        o_split = sem("o_split")
        att_done = sem("o_att_done")
        x1_done = sem("o_x1_done")
        stats_done = sem("o_stats_done")
        mean_var_done = sem("o_mean_var_done")
        var_eps_done = sem("o_var_eps_done")
        std_done = sem("o_std_done")
        rstd_done = sem("o_rstd_done")
        xn_done = sem("o_xn_done")
        x2_turned = sem("o_x2_turned")
        x2_raw_done = sem("o_x2_raw_done")
        x2_split = sem("o_x2_split")
        g_done = sem("o_g_done")
        logits_done = sem("o_logits_done")
        rank_step = sem("o_rank_step")
        weight_done = sem("o_weight_done")
        we_loaded = [sem(f"e_w_loaded{s}") for s in range(2)]
        b_loaded = [sem(f"e_b_loaded{s}") for s in range(2)]
        we_hi_done = sem("e_w_hi_done")
        we_split = sem("e_w_split")
        y_done = sem("e_y_done")
        z_done = sem("e_z_done")
        r_done = sem("e_r_done")
        added = sem("e_added")
        stored = sem("e_stored")

        def expert_w(s):
            return slice(s * NC, (s + 1) * NC)

        block = ctx.enter_context(nc.Block())
        steps = range(-3, NT + 1)

        @block.sync
        def _(sp):
            def load_o(n):
                sp.dma_start(o_raw[:, n % 2, :, :], o_v[:, :, n * P:(n + 1) * P]).then_inc(o_loaded[n % 2], 16)

            def load_x(n):
                sp.dma_start(x_sb[:, n % 2, :], x_v[n]).then_inc(x_loaded[n % 2], 16)

            def load_wo(n):
                sp.dma_start(wo_raw[:, n % 2, :, :], wo_v[:, n * KP:(n + 1) * KP, :]).then_inc(wo_loaded[n % 2], 16)

            load_wo(0)
            load_o(0)
            load_wo(1)
            load_o(1)
            load_x(0)
            load_x(1)
            sp.dma_start(wg_sb[:], wg.rearrange("(c p) e -> p c e", p=P)).then_inc(wg_loaded, 16)
            for n in range(2, PARTS):
                sp.wait_ge(wo_split, n - 1)
                load_wo(n)
            sp.dma_start(bg_bc[:], bg.partition_broadcast(P)).then_inc(const_loaded, 16)
            sp.dma_start(earlier[:], earlier_in.rearrange("p (e j) -> p e j", e=E)).then_inc(const_loaded, 16)
            for n in range(2, NT):
                sp.wait_ge(o_split, n - 1)
                load_o(n)
                sp.wait_ge(x1_done, n - 1)
                load_x(n)
            with sp.Fori(0, E // 2) as pair:
                for s in range(2):
                    e = pair * 2 + s
                    sp.wait_ge(we_split, T0 + e - 1)
                    sp.dma_start(we_raw[:, s, :, :], we_v[:, bass.ds(e * NC, NC), :]).then_inc(we_loaded[s], 16)
                    sp.wait_ge(z_done, E0 + (e - 1) * NT)
                    sp.dma_start(b_bc[:, s, :], be[bass.ds(e, 1), :].squeeze(0).partition_broadcast(P)).then_inc(b_loaded[s], 16)
            for t in range(NT):
                sp.wait_ge(added, T0 + (E - 1) * NT + t + 1)
                sp.dma_start(out_v[t], x1[:, t, :]).then_inc(stored, 16)
            sp.wait_ge(stored, 16 * NT)

        @block.scalar
        def _(act):
            act.sem_inc(r_done, T0)

            def round_wo(n):
                act.wait_ge(wo_loaded[n % 2], 16 * (n // 2 + 1))
                nc.scalar.activation(w_hi[:, n * KP:(n + 1) * KP, :], wo_raw[:, n % 2, :, :], ACT.Copy).then_inc(wo_hi_done, 1)

            round_wo(0)
            for n in steps:
                if 0 <= n < NT:
                    act.wait_ge(x2_turned, n + 1)
                    nc.scalar.activation(x2_hi[:, :, n * P:(n + 1) * P], x2_at[n % 2], ACT.Copy)
                    if n >= 2:
                        act.wait_ge(g_done, n - 1)
                    nc.scalar.activation(x2_raw[:, n % 2, :, :], x2_at[n % 2], ACT.Copy).then_inc(x2_raw_done, 1)
                if 0 <= n + 1 < NT:
                    act.wait_ge(var_eps_done, n + 2)
                    nc.scalar.activation(std[:, n + 1:n + 2], var_eps[:, n + 1:n + 2], ACT.Sqrt).then_inc(std_done, 1)
                if n + 3 < NT:
                    act.wait_ge(o_loaded[(n + 3) % 2], 16 * ((n + 3) // 2 + 1))
                    if n + 3 >= 2:
                        act.wait_ge(att_done, n + 2)
                    nc.scalar.activation(o_hi[:, (n + 3) % 2, :, :], o_raw[:, (n + 3) % 2, :, :], ACT.Copy).then_inc(o_hi_done, 1)
                if n == steps[0]:
                    for k in range(1, PARTS):
                        round_wo(k)
            act.wait_ge(att_done, NT)

            def round_we(e, s):
                act.wait_ge(we_loaded[s], (e - s) * 8 + 16)
                act.wait_ge(y_done, E0 + (e - 1) * NT)
                nc.scalar.activation(w_hi[:, expert_w(s), :], we_raw[:, s, :, :], ACT.Copy).then_inc(we_hi_done, 1)

            def pair_of(e0, more):
                for s in range(2):
                    for t in range(NT):
                        if t == 1 and (s == 0 or more):
                            round_we(e0 + s + 1, 1 - s)
                        n = (e0 + s) * NT + t
                        act.wait_ge(z_done, E0 + n + 1)
                        act.wait_ge(added, T0 + n - 1)
                        nc.scalar.activation(r[:, t % 2, :], z[:, t % 2, :], ACT.Relu,
                                             scale=weight[:, bass.ds(e0 + (t * E + s), 1)]).then_inc(r_done, 1)

            round_we(0, 0)
            act.wait_ge(weight_done, 1)
            with act.Fori(0, E // 2 - 1) as pair:
                pair_of(pair * 2, True)
            pair_of(E - 2, False)

        @block.vector
        def _(dve):
            dve.sem_inc(z_done, E0)
            dve.sem_inc(added, T0)
            dve.sem_inc(we_split, T0)

            def split_wo(n):
                part = slice(n * KP, (n + 1) * KP)
                dve.wait_ge(wo_hi_done, n + 1)
                nc.vector.tensor_tensor(w_lo[:, part, :], wo_raw[:, n % 2, :, :], w_hi[:, part, :], ALU.subtract).then_inc(wo_split, 1)

            split_wo(0)
            for n in steps:
                i = n + 1
                if 0 <= i < NT:
                    dve.wait_ge(att_done, i + 1)
                    dve.wait_ge(x_loaded[i % 2], 16 * (i // 2 + 1))
                    nc.vector.tensor_tensor(x1[:, i, :], y_at[i % 2], x_sb[:, i % 2, :], ALU.add).then_inc(x1_done, 1)
                    dve.wait_ge(x1_done, i + 1)
                    nc.vector.bn_stats(stats[:, i, :], x1[:, i, :]).then_inc(stats_done, 1)
                    dve.wait_ge(stats_done, i + 1)
                    nc.vector.bn_aggr(mean_var[:, i, :], stats[:, i, :]).then_inc(mean_var_done, 1)
                    dve.wait_ge(mean_var_done, i + 1)
                    nc.vector.tensor_scalar_add(var_eps[:, i:i + 1], mean_var[:, i, 1:2], EPS).then_inc(var_eps_done, 1)
                if 0 <= n < NT:
                    dve.wait_ge(x2_raw_done, n + 1)
                    tok = slice(n * P, (n + 1) * P)
                    nc.vector.tensor_tensor(x2_lo[:, :, tok], x2_at[n % 2], x2_hi[:, :, tok], ALU.subtract).then_inc(x2_split, 1)
                if 0 <= i < NT:
                    dve.wait_ge(std_done, i + 1)
                    nc.vector.reciprocal(rstd[:, i:i + 1], std[:, i:i + 1]).then_inc(rstd_done, 1)
                    dve.wait_ge(rstd_done, i + 1)
                    if i >= 2:
                        dve.wait_ge(x2_turned, i - 1)
                    nc.vector.tensor_scalar(xn[:, i % 2, :], x1[:, i, :], mean_var[:, i, 0:1], rstd[:, i:i + 1],
                                            ALU.subtract, ALU.mult).then_inc(xn_done, 1)
                if n >= 1:
                    if n == 1:
                        dve.wait_ge(const_loaded, 32)
                    dve.wait_ge(g_done, n)
                    nc.vector.tensor_tensor(logits[:, n - 1, :], g_at[(n - 1) % 2], bg_bc[:], ALU.add).then_inc(logits_done, 1)
                if n + 3 < NT:
                    s = (n + 3) % 2
                    dve.wait_ge(o_hi_done, n + 4)
                    nc.vector.tensor_tensor(o_lo[:, s, :, :], o_raw[:, s, :, :], o_hi[:, s, :, :], ALU.subtract).then_inc(o_split, 1)
                if n == steps[0]:
                    for k in range(1, PARTS):
                        split_wo(k)
            dve.wait_ge(logits_done, NT)
            shape = [P, NT, E, E]
            of_other = logits[:].rearrange("p t (o j) -> p t o j", o=1).to_broadcast(shape)
            of_this = logits[:].rearrange("p t (e o) -> p t e o", o=1).to_broadcast(shape)
            nc.vector.tensor_tensor(above[:], of_other, of_this, ALU.is_gt).then_inc(rank_step, 1)
            nc.vector.tensor_tensor(same[:], of_other, of_this, ALU.is_equal).then_inc(rank_step, 1)
            dve.wait_ge(rank_step, 2)
            before = earlier[:].rearrange("p (o e) j -> p o e j", o=1).to_broadcast(shape)
            nc.vector.tensor_tensor(same[:], same[:], before, ALU.mult).then_inc(rank_step, 1)
            dve.wait_ge(rank_step, 3)
            nc.vector.tensor_tensor(above[:], above[:], same[:], ALU.add).then_inc(rank_step, 1)
            dve.wait_ge(rank_step, 4)
            nc.vector.reduce_sum(rank[:], above[:], AX_X).then_inc(rank_step, 1)
            dve.wait_ge(rank_step, 5)
            nc.vector.tensor_scalar(weight[:], rank[:].rearrange("p t e -> p (t e)"), TOP_K - 0.5, 1.0 / TOP_K,
                                    ALU.is_lt, ALU.mult).then_inc(weight_done, 1)

            def split_we(e, s):
                dve.wait_ge(we_hi_done, e + 1)
                nc.vector.tensor_tensor(w_lo[:, expert_w(s), :], we_raw[:, s, :, :], w_hi[:, expert_w(s), :],
                                        ALU.subtract).then_inc(we_split, 1)

            def add_bias(n, s, t):
                dve.wait_ge(y_done, E0 + n + 1)
                dve.wait_ge(r_done, T0 + n - 1)
                nc.vector.tensor_tensor(z[:, t % 2, :], ps[:, t, :], b_bc[:, s, :], ALU.add).then_inc(z_done, 1)

            def accumulate(n, t):
                dve.wait_ge(r_done, T0 + n + 1)
                nc.vector.tensor_tensor(x1[:, t, :], x1[:, t, :], r[:, t % 2, :], ALU.add).then_inc(added, 1)

            def pair_of(e0, more):
                for s in range(2):
                    e = e0 + s
                    dve.wait_ge(b_loaded[s], e0 * 8 + 16)
                    for t in range(NT):
                        add_bias(e * NT + t, s, t)
                        if t > 0:
                            accumulate(e * NT + t - 1, t - 1)
                        if t == 1 and (s == 0 or more):
                            split_we(e + 1, 1 - s)
                    accumulate(e * NT + NT - 1, NT - 1)

            split_we(0, 0)
            with dve.Fori(0, E // 2 - 1) as pair:
                pair_of(pair * 2, True)
            pair_of(E - 2, False)

        @block.tensor
        def _(pe):
            pe.sem_inc(y_done, E0)

            def route(n):
                pe.wait_ge(x2_raw_done, n + 1)
                if n == 0:
                    pe.wait_ge(wg_loaded, 16)
                if n >= 2:
                    pe.wait_ge(logits_done, n - 1)
                for c in range(NC):
                    last = nc.tensor.matmul(g_at[n % 2], x2_raw[:, n % 2, c, :], wg_sb[:, c, :], start=(c == 0), stop=(c == NC - 1))
                last.then_inc(g_done, 1)

            for n in steps:
                if 0 <= n < NT:
                    pe.wait_ge(xn_done, n + 1)
                    if n >= 2:
                        pe.wait_ge(x2_split, n - 1)
                    for c in range(NC):
                        last = nc.tensor.transpose(x2_at[n % 2][:, c, :], xn[:, n % 2, c * P:(c + 1) * P], ident[:])
                    last.then_inc(x2_turned, 1)
                if n >= 1:
                    route(n - 1)
                i = n + 2
                if 0 <= i < NT:
                    pe.wait_ge(o_split, i + 1)
                    if i >= 2:
                        pe.wait_ge(x1_done, i - 1)
                    for part in range(PARTS):
                        if i == 0:
                            pe.wait_ge(wo_split, part + 1)
                        for k in range(part * KP, (part + 1) * KP):
                            for m, (stationary, moving) in enumerate(three_passes(
                                    o_hi[:, i % 2, k, :], o_lo[:, i % 2, k, :], w_hi[:, k, :], w_lo[:, k, :])):
                                last = nc.tensor.matmul(y_at[i % 2], stationary, moving,
                                                        start=(k == 0 and m == 0), stop=(k == NK - 1 and m == 2))
                    last.then_inc(att_done, 1)

            def pair_of(e0):
                for s in range(2):
                    e = e0 + s
                    pe.wait_ge(we_split, T0 + e + 1)
                    for t in range(NT):
                        tok = slice(t * P, (t + 1) * P)
                        pe.wait_ge(z_done, E0 + (e - 1) * NT + t + 1)
                        split_product(nc, ps[:, t, :], [(x2_hi[:, c, tok], x2_lo[:, c, tok], w_hi[:, s * NC + c, :], w_lo[:, s * NC + c, :])
                                                        for c in range(NC)]).then_inc(y_done, 1)

            pe.wait_ge(x2_split, NT)
            pe.wait_ge(logits_done, NT)
            with pe.Fori(0, E // 2) as pair:
                pair_of(pair * 2)


TOP_K = 2
HEADS, GROUPS, HEAD_DIM = 16, 4, 96


def cross_attention_and_experts(nc, x, ctx_t, wq, wk, wv, wo, wg, bg, we, be, ident, earlier, out, queries):
    T, D = x.shape
    B = ctx_t.shape[0]
    G = HEADS // GROUPS
    NC, KVD = D // P, GROUPS * HEAD_DIM
    xt_dram = nc.dram_tensor("normed_latents_t", (D, T), F32).ap()
    q_dram = nc.dram_tensor("queries_t", (HEADS * HEAD_DIM, T), F32).ap()
    l_dram = nc.dram_tensor("softmax_sums", (G * queries,), F32).ap()
    o_dram = nc.dram_tensor("attended_t", (HEADS * HEAD_DIM, T), F32).ap()
    with nc.sbuf_tensor("identity_sb", [P, P], F32) as ident_sb:
        with (
            nc.sbuf_tensor("wk_hi", [P, NC, KVD], F32R) as wk_hi,
            nc.sbuf_tensor("wk_lo", [P, NC, KVD], F32R) as wk_lo,
            nc.sbuf_tensor("wv_hi", [P, NC, KVD], F32R) as wv_hi,
            nc.sbuf_tensor("wv_lo", [P, NC, KVD], F32R) as wv_lo,
            nc.sbuf_tensor("landing", [P, 2, NC, KVD], F32) as landing,
        ):
            wkv = (wk_hi, wk_lo, wv_hi, wv_lo)
            latent_norm_and_queries(nc, x, wq, wk, wv, ident, xt_dram, q_dram, wkv, ident_sb, landing)
            attention(nc, ctx_t, wkv, ident_sb, landing, xt_dram, q_dram, l_dram, o_dram, B, GROUPS, HEAD_DIM, G, queries)
        output_router_experts(nc, x, wo, wg, bg, we, be, earlier, ident_sb, o_dram, out)


def kernel(x, ctx_4096, L0_xattn_Wq, L0_xattn_Wk, L0_xattn_Wv, L0_xattn_Wo, L0_ffn_W_gate, L0_ffn_b_gate,
           L0_ffn_W_e, L0_ffn_b_e):
    import numpy as np
    import concourse.bacc as bacc
    from concourse.bass_utils import run_bass_kernel_spmd

    B, Q, D = x.shape
    E = L0_ffn_W_gate.shape[1]
    arrays = {
        "x": np.reshape(x, (B * Q, D)),
        "context_t": np.transpose(ctx_4096, (0, 2, 1)),
        "wq_t": np.transpose(L0_xattn_Wq),
        "wk_t": np.transpose(L0_xattn_Wk),
        "wv_t": np.transpose(L0_xattn_Wv),
        "wo_t": np.transpose(L0_xattn_Wo),
        "w_gate": L0_ffn_W_gate,
        "b_gate": L0_ffn_b_gate,
        "w_e": L0_ffn_W_e,
        "b_e": L0_ffn_b_e,
        "identity": np.eye(P, dtype=np.float32),
        "earlier": np.broadcast_to(np.tril(np.ones((E, E), np.float32), -1).reshape(1, E * E), (P, E * E)),
    }
    arrays = {name: np.ascontiguousarray(a) for name, a in arrays.items()}
    nc = bacc.Bacc("TRN2", target_bir_lowering=False, num_devices=1)
    args = [nc.dram_tensor(name, a.shape, mybir.dt.from_np(a.dtype), kind="ExternalInput").ap()
            for name, a in arrays.items()]
    out = nc.dram_tensor("out", (B * Q, D), F32, kind="ExternalOutput").ap()
    cross_attention_and_experts(nc, *args, out, Q)
    result = run_bass_kernel_spmd(nc, [arrays], core_ids=[0])
    return np.reshape(result.results[0]["out"], (B, Q, D))
```

```python
from contextlib import ExitStack

import concourse.bass as bass
from concourse import mybir

F32 = mybir.dt.float32
F32R = mybir.dt.float32r
ALU = mybir.AluOpType
ACT = mybir.ActivationFunctionType
AX_X = mybir.AxisListType.X

P = 128
BANK = 512
EPS = 1e-5


def three_passes(w_hi, w_lo, m_hi, m_lo):
    return ((w_hi, m_hi), (w_hi, m_lo), (w_lo, m_hi))


def split_product(nc, out, blocks, between=()):
    between = list(between)
    total = len(between)
    pairs = [pair for block in blocks for pair in three_passes(*block)]
    for n, (stationary, moving) in enumerate(pairs):
        last = nc.tensor.matmul(out, stationary, moving, start=(n == 0), stop=(n == len(pairs) - 1))
        while between and n + 1 >= len(pairs) * (total - len(between) + 1) // (total + 1):
            between.pop(0)()
    return last


def key_rows(kvd):
    hd = kvd // GROUPS
    tail = P - hd
    assert (GROUPS - 1) * tail == hd and (GROUPS - 1) * P == kvd and hd % 32 == 0 and tail == 32
    return hd, tail


def chunk_at(work, part, c, GQ, NC, CW):
    at = GQ + c % 2 * NC * CW
    return work[:, part, at:at + NC * CW].rearrange("p (c s) -> p c s", c=NC)


def latent_norm_and_queries(nc, x, ctx_t, wq, wk, wv, ident_in, xt_dram, q_dram, wkv, ident, landing, work, q_raw,
                            q_sb, q_stored, GQ):
    T, D = x.shape
    QD, KVD = wq.shape[1], wk.shape[1]
    NT, NC, NM = T // P, D // P, QD // P
    HALVES = T // BANK
    WCOLS = landing.shape[3]
    NQW = QD // WCOLS
    BLOCKS = WCOLS // P
    NB = 4
    TURNS = 4
    NS = len(q_stored)
    x_v = x.rearrange("(t p) d -> p t d", p=P)
    wq_v = wq.rearrange("(c p) m -> p c m", p=P)
    wk_v = wk.rearrange("(c p) m -> p c m", p=P)
    wv_v = wv.rearrange("(c p) m -> p c m", p=P)
    xt_v = xt_dram.rearrange("(c p) t -> p c t", p=P)
    ctx_v = ctx_t[0].rearrange("(c p) s -> p c s", p=P)
    HD, TAIL = key_rows(KVD)

    with ExitStack() as ctx:
        def sb(name, shape, dt=F32):
            return ctx.enter_context(nc.sbuf_tensor(name, shape, dt))

        def sem(name):
            return ctx.enter_context(nc.semaphore(name))

        x_sb = sb("n1_x", [P, NT, D])
        stats = sb("n1_stats", [P, NT, 6])
        mean_var = sb("n1_mean_var", [P, NT, 2])
        eps = sb("n1_eps", [P, 1])
        std = sb("n1_std", [P, NT])
        rstd = sb("n1_rstd", [P, NT])
        xn = sb("n1_xn", [P, TURNS, D])
        xt_hi = sb("n1_xt_hi", [P, NC, T], F32R)
        xt_lo = sb("n1_xt_lo", [P, NC, T], F32R)
        xt_raw = sb("n1_xt_raw", [P, 2, NC, P])
        wq_hi = sb("q_w_hi", [P, NQW, NC, WCOLS], F32R)
        wq_lo = sb("q_w_lo", [P, NQW, NC, WCOLS], F32R)
        xt_ps = ctx.enter_context(nc.psum_tensor("n1_xt_ps", [P, TURNS, NC, P], F32))
        q_ps = ctx.enter_context(nc.psum_tensor("q_ps", [P, NB, BANK], F32))
        wk_hi, wk_lo, wv_hi, wv_lo = wkv
        chunks = [[chunk_at(work, part, c, GQ, NC, WCOLS) for c in range(H_AHEAD)] for part in (0, 1)]
        parts_hi = [wq_hi[:, n, :, :] for n in range(NQW)] + [wk_hi[:], wv_hi[:]] + chunks[0]
        parts_lo = [wq_lo[:, n, :, :] for n in range(NQW)] + [wk_lo[:], wv_lo[:]] + chunks[1]
        NW = len(parts_hi)
        AT = BANK // P
        ROUND_AT = {2: 2, 3: 5, 4: 8, 5: 10, 6: 12, 7: 14}
        assert set(ROUND_AT) == set(range(2, NW))

        x_loaded = [sem(f"n1_x_loaded{t}") for t in range(NT)]
        ident_loaded = sem("n1_ident_loaded")
        stats_done = sem("n1_stats_done")
        mean_var_done = sem("n1_mean_var_done")
        eps_set = sem("n1_eps_set")
        std_done = sem("n1_std_done")
        rstd_done = sem("n1_rstd_done")
        xn_done = sem("n1_xn_done")
        xt_done = sem("n1_xt_done")
        xt_hi_done = sem("n1_xt_hi_done")
        xt_raw_done = sem("n1_xt_raw_done")
        xt_split = sem("n1_xt_split")
        xt_stored = [sem(f"n1_xt_stored{s}") for s in range(2)]
        w_loaded = [sem(f"q_w_loaded{s}") for s in range(2)]
        w_hi_done = sem("q_w_hi_done")
        w_split = sem("q_w_split")
        first_w_split = sem("q_first_w_split")
        q_done = sem("q_done")
        q_copied = sem("q_copied")
        first_q_loaded = sem("q_first_q_loaded")

        block = ctx.enter_context(nc.Block())
        groups = [(m, half) for half in range(HALVES) for m in range(NM)]

        @block.sync
        def _(sp):
            def load_x(t):
                sp.dma_start(x_sb[:, t, :], x_v[:, t, :]).then_inc(x_loaded[t], 16)

            def load_w(n):
                dst = landing[:, n % 2, :, :]
                if n < NQW:
                    sp.dma_start(dst, wq_v[:, :, n * WCOLS:(n + 1) * WCOLS]).then_inc(w_loaded[n % 2], 16)
                elif n == NQW:
                    for m in range(BLOCKS):
                        sp.dma_start(dst[:, :, m * P:m * P + HD], wk_v[:, :, m * HD:(m + 1) * HD]).then_inc(w_loaded[n % 2], 16)
                        sp.dma_start(dst[:, :, m * P + HD:(m + 1) * P],
                                     wk_v[:, :, BLOCKS * HD + m * TAIL:BLOCKS * HD + (m + 1) * TAIL]).then_inc(w_loaded[n % 2], 16)
                elif n == NQW + 1:
                    sp.dma_start(dst, wv_v).then_inc(w_loaded[n % 2], 16)
                else:
                    c = n - NQW - 2
                    sp.dma_start(dst, ctx_v[:, :, c * WCOLS:(c + 1) * WCOLS]).then_inc(w_loaded[n % 2], 16)

            load_x(0)
            sp.dma_start(ident[:], ident_in).then_inc(ident_loaded, 16)
            for t in range(1, AT):
                load_x(t)
            load_w(0)
            for t in range(AT, NT):
                load_x(t)
            load_w(1)
            sp.wait_ge(first_w_split, BLOCKS)
            load_w(2)
            sp.wait_ge(w_split, 1)
            load_w(3)
            for n, (m, half) in enumerate(groups):
                for k in range(4, NW):
                    if ROUND_AT[k - 2] == n - 1:
                        sp.wait_ge(w_split, k - 2)
                        load_w(k)
                sp.wait_ge(q_copied, n + 1)
                sp.dma_start(q_dram[m * P:(m + 1) * P, half * BANK:(half + 1) * BANK], q_sb[:, n % NS, :]).then_inc(q_stored[n % NS], 16)

        @block.gpsimd
        def _(pool):
            pool.wait_ge(w_hi_done, 1)
            for m in range(BLOCKS):
                cols = slice(m * P, (m + 1) * P)
                nc.gpsimd.tensor_tensor(parts_lo[0][:, :, cols], landing[:, 0, :, cols], parts_hi[0][:, :, cols],
                                        ALU.subtract).then_inc(first_w_split, 1)
            for t in range(NT):
                pool.wait_ge(xt_split, t + 1)
                if t >= 2:
                    pool.wait_ge(xt_stored[t % 2], 16 * (t // 2))
                tok = slice(t * P, (t + 1) * P)
                nc.gpsimd.tensor_tensor(xt_raw[:, t % 2, :, :], xt_hi[:, :, tok], xt_lo[:, :, tok], ALU.add).then_inc(xt_raw_done, 1)
                pool.wait_ge(xt_raw_done, t + 1)
                pool.dma_start(xt_v[:, :, tok], xt_raw[:, t % 2, :, :]).then_inc(xt_stored[t % 2], 16)
            for s in range(2):
                pool.wait_ge(xt_stored[s], 16 * NT // 2)
            G, Q = q_raw.shape[1:]
            for n in range(NS):
                pool.wait_ge(q_stored[n], 16 * NM // NS)
            pool.dma_start(q_raw[:], q_dram.rearrange("(h d) t -> d h t", d=HD)[:, 0:G, 0:Q]).then_inc(first_q_loaded, 16)
            pool.wait_ge(first_q_loaded, 16)

        def w_loads(n):
            return 16 * sum(2 * BLOCKS if i == NQW else 1 for i in range(n % 2, n + 1, 2))

        @block.vector
        def _(dve):
            def measure(t):
                dve.wait_ge(x_loaded[t], 16)
                nc.vector.bn_stats(stats[:, t, :], x_sb[:, t, :]).then_inc(stats_done, 1)
                dve.wait_ge(stats_done, t + 1)
                nc.vector.bn_aggr(mean_var[:, t, :], stats[:, t, :]).then_inc(mean_var_done, 1)

            def norm(t):
                dve.wait_ge(std_done, t + 1)
                nc.vector.reciprocal(rstd[:, t:t + 1], std[:, t:t + 1]).then_inc(rstd_done, 1)
                dve.wait_ge(rstd_done, t + 1)
                if t >= TURNS:
                    dve.wait_ge(xt_done, t - TURNS + 1)
                nc.vector.tensor_scalar(xn[:, t % TURNS, :], x_sb[:, t, :], mean_var[:, t, 0:1], rstd[:, t:t + 1],
                                        ALU.subtract, ALU.mult).then_inc(xn_done, 1)

            def split(t):
                dve.wait_ge(xt_hi_done, t + 1)
                nc.vector.tensor_tensor(xt_lo[:, :, t * P:(t + 1) * P], xt_ps[:, t % TURNS, :, :],
                                        xt_hi[:, :, t * P:(t + 1) * P], ALU.subtract).then_inc(xt_split, 1)

            def split_w(n):
                dve.wait_ge(w_hi_done, n + 1)
                nc.vector.tensor_tensor(parts_lo[n], landing[:, n % 2, :, :], parts_hi[n], ALU.subtract).then_inc(w_split, 1)

            nc.vector.memset(eps[:], EPS).then_inc(eps_set, 1)
            for t in range(AT):
                measure(t)
                if t >= 1:
                    norm(t - 1)
            norm(AT - 1)
            for t in range(AT):
                split(t)
            for t in range(AT, NT):
                measure(t)
                norm(t)
                if t == AT:
                    split_w(1)
                else:
                    split(t - 1)
            split(NT - 1)
            for n in range(2, NW):
                split_w(n)

        @block.scalar
        def _(act):
            def round_w(n):
                act.wait_ge(w_loaded[n % 2], w_loads(n))
                nc.scalar.activation(parts_hi[n], landing[:, n % 2, :, :], ACT.Copy).then_inc(w_hi_done, 1)

            def copy_q(n):
                act.wait_ge(q_done, n + 1)
                if n >= NS:
                    act.wait_ge(q_stored[n % NS], 16 * (n // NS))
                nc.scalar.activation(q_sb[:, n % NS, :], q_ps[:, n % NB, :], ACT.Copy).then_inc(q_copied, 1)

            def root(t):
                act.wait_ge(mean_var_done, t + 1)
                nc.scalar.activation(std[:, t:t + 1], mean_var[:, t, 1:2], ACT.Sqrt, bias=eps[:]).then_inc(std_done, 1)

            def round_x(t):
                act.wait_ge(xt_done, t + 1)
                nc.scalar.activation(xt_hi[:, :, t * P:(t + 1) * P], xt_ps[:, t % TURNS, :, :], ACT.Copy).then_inc(xt_hi_done, 1)

            act.wait_ge(eps_set, 1)
            for t in range(AT):
                root(t)
            for t in range(AT):
                round_x(t)
                if t == 1:
                    round_w(0)
            root(AT)
            round_w(1)
            for n in range(len(groups)):
                for k in range(2, NW):
                    if ROUND_AT[k] == n:
                        round_w(k)
                copy_q(n)
                t = AT + n
                if t + 1 < NT:
                    root(t + 1)
                if t < NT:
                    round_x(t)

        @block.tensor
        def _(pe):
            def turn(t):
                pe.wait_ge(xn_done, t + 1)
                if t >= TURNS:
                    pe.wait_ge(xt_split, t - TURNS + 1)
                for c in range(NC):
                    last = nc.tensor.transpose(xt_ps[:, t % TURNS, c, :], xn[:, t % TURNS, c * P:(c + 1) * P], ident[:])
                last.then_inc(xt_done, 1)

            pe.wait_ge(ident_loaded, 16)
            for t in range(AT):
                turn(t)
            for n, (m, half) in enumerate(groups):
                part, i = divmod(m, BLOCKS)
                if m == 0:
                    pe.wait_ge(xt_split, AT * (half + 1))
                if m < BLOCKS and half == 0:
                    pe.wait_ge(first_w_split, m + 1)
                elif i == 0 and half == 0:
                    pe.wait_ge(w_split, part)
                if n >= NB:
                    pe.wait_ge(q_copied, n - NB + 1)
                rows, cols = slice(i * P, (i + 1) * P), slice(half * BANK, (half + 1) * BANK)
                split_product(nc, q_ps[:, n % NB, :],
                              [(wq_hi[:, part, c, rows], wq_lo[:, part, c, rows], xt_hi[:, c, cols], xt_lo[:, c, cols])
                               for c in range(NC)]).then_inc(q_done, 1)
                if AT + n < NT:
                    turn(AT + n)


def output_weights(wkv, KP, D):
    wk_hi, wk_lo, wv_hi, wv_lo = [w[:].rearrange("p c m -> p (c m)").rearrange("p (k d) -> p k d", k=KP) for w in wkv]
    return [(wk_hi, wk_lo), (wv_hi, wv_lo)]


def landed(landing, s, KP, D):
    return landing[:, s, :, :].rearrange("p c m -> p (c m)").rearrange("p (k d) -> p k d", k=KP)


def attended_tile(v, s, NK):
    return v[:].rearrange("p t k r -> p t (k r)")[:, 0:NK, s * P:(s + 1) * P]


def attention(nc, ctx_t, wo, wkv, ident, h_raw, work, q_raw, q_stored, values_sb, tail, banks, xt_dram, q_dram, l_dram, o_dram,
              B, KV, HD, G, Q):
    CTX = ctx_t.shape[2]
    D = ctx_t.shape[1]
    NC = D // P
    S = CTX + Q
    CW = 3 * P
    CHUNKS = [(s0, min(CW, S - s0)) for s0 in range(0, S, CW)]
    TILES = [(s0, min(P, S - s0)) for s0 in range(0, S, P)]
    NCH, NTL = len(CHUNKS), len(TILES)
    SE = S + S % 2
    GQ = G * Q
    NJ = GQ // P
    QS = G * HD
    R = HD + 1
    SCALE = float(HD) ** -0.5
    KVD = KV * HD
    HV = GQ // BANK
    NG = KV * NTL
    BLOCKS = KVD // P
    TAIL = P - HD
    PC = BLOCKS + CW // P
    NPR = PC * NCH
    LAST_KEYS = PC * (NCH - 1) - 1
    NJB = NJ * NCH
    JOBS_AT, JOBS_PER = 3, 4
    M_AT = JOBS_AT + NJB // JOBS_PER
    INVERT_AT = 5
    CREDIT = 3
    assert NPR % 6 == 0 and NG % PSLOTS == 0 and KVD == CW and GQ == 2 * BANK and NJB % 2 == 0
    assert 2 * NC * CW == (PSLOTS - 1) * GQ and M_AT < NTL - 1

    NK = KV * G * HD // P
    KP = NK // PARTS
    WO_AHEAD, O_AHEAD, PIECES_AT = 2, 2, 3
    WO_PIECES, O_PIECES = WO_AHEAD * KP, O_AHEAD * KP
    OK = NK // KP
    assert PIECES_AT + WO_PIECES + O_PIECES <= NTL and O_AHEAD * P <= (KV - 1) * R

    wk_hi, wk_lo, wv_hi, wv_lo = wkv
    v_hi, v_lo = values_sb
    o_sb, l_rows, l_inv, l_bc = tail
    wo_v = wo.rearrange("(k p) d -> p k d", p=P)
    o_tiles = o_dram.rearrange("(k p) t -> p k t", p=P)
    wo_at = output_weights(wkv, KP, D)
    ctx_v = ctx_t.rearrange("b (c p) s -> p (b c) s", p=P)
    xt_v = xt_dram.rearrange("(c p) t -> p c t", p=P)
    q_v = q_dram.rearrange("(h d) t -> d h t", d=HD)
    o_v = o_dram.rearrange("(h d) t -> d h t", d=HD)

    with ExitStack() as ctx:
        def sb(name, shape, dt=F32):
            return ctx.enter_context(nc.sbuf_tensor(name, shape, dt))

        def sem(name):
            return ctx.enter_context(nc.semaphore(name))

        kt_hi = sb("a_kt_hi", [R, KV, SE], F32R)
        kt_lo = sb("a_kt_lo", [R, KV, SE], F32R)
        q_hi = sb("a_q_hi", [R, 2, GQ], F32R)
        q_lo = sb("a_q_lo", [HD, 2, GQ], F32R)
        table = sb("a_table", [1, 1])
        m_part = sb("a_m_part", [P, NJ, NCH])
        m_all = sb("a_m_all", [P, NJ])
        m_row = sb("a_m_row", [NJ, P], F32R)
        s_ps = banks[:, 0:2 * HV, :].rearrange("p (s a) n -> p s a n", s=2)
        o_ps = banks[:, 2 * HV:3 * HV, :]
        m_ps = banks[:, 3 * HV:3 * HV + 2, :]
        pr_ps = [s_ps[:, n // 2, n % 2, :] for n in range(4)] + [o_ps[:, n, :] for n in range(2)]
        NB = len(pr_ps)

        def h_at(part, c):
            return chunk_at(work, part, c, GQ, NC, CW)

        def p_at(part, g):
            return work[:, part, g % PSLOTS * GQ:(g % PSLOTS + 1) * GQ]

        ones_set = sem("a_ones_set")
        table_set = sem("a_table_set")
        h_loaded = [sem(f"a_h_loaded{s}") for s in range(2)]
        h_hi_done = sem("a_h_hi_done")
        h_split = sem("a_h_split")
        pr_done = sem("a_pr_done")
        pr_hi_done = sem("a_pr_hi_done")
        pr_split = sem("a_pr_split")
        q_loaded = sem("a_q_loaded")
        q_hi_done = sem("a_q_hi_done")
        q_split = sem("a_q_split")
        mm_done = sem("a_mm_done")
        mm_reduced = sem("a_mm_reduced")
        m_all_done = sem("a_m_all_done")
        m_turned = sem("a_m_turned")
        m_row_done = sem("a_m_row_done")
        m_row_placed = sem("a_m_row_placed")
        s_done = sem("a_s_done")
        exp_done = sem("a_exp_done")
        exp_half_done = sem("a_exp_half_done")
        p_split = sem("a_p_split")
        p_half_split = sem("a_p_half_split")
        pv_done = sem("a_pv_done")
        o_copied = sem("a_o_copied")
        l_moved = sem("a_l_moved")
        l_stored = sem("a_l_stored")
        l_spread = sem("a_l_spread")
        l_inverted = sem("a_l_inverted")
        o_normed = sem("a_o_normed")
        o_stored = sem("a_o_stored")
        o_sb_free = sem("a_o_sb_free")
        wo_loaded = sem("a_wo_loaded")
        wo_rest_loaded = sem("a_wo_rest_loaded")
        tile_loaded = sem("a_tile_loaded")
        piece_hi_done = sem("a_piece_hi_done")
        piece_split = sem("a_piece_split")

        def piece(t):
            n = t - PIECES_AT
            if 0 <= n < WO_PIECES:
                part, k = divmod(n, KP)
                hi, lo = wo_at[part]
                return "weights", landed(h_raw, part, KP, D)[:, k, :], hi[:, k, :], lo[:, k, :]
            if 0 <= n - WO_PIECES < O_PIECES:
                slot, k = divmod(n - WO_PIECES, KP)
                rows = slice(k * OK, (k + 1) * OK)
                hi, lo = attended_tile(v_hi, slot, NK)[:, rows, :], attended_tile(v_lo, slot, NK)[:, rows, :]
                return "tile", lo.bitcast(F32), hi, lo
            return None

        def jobs_of(g):
            kv, t = divmod(g, NTL)
            if kv + 1 >= KV or not JOBS_AT <= t < M_AT:
                return []
            n0 = (t - JOBS_AT) * JOBS_PER
            return [(kv + 1, n) for n in range(n0, n0 + JOBS_PER)]

        def projections():
            items = []
            for c in range(NCH):
                items += [("k", c, m) for m in range(BLOCKS)]
                items += [("v", c, CW // P * c + i) for i in range(CW // P)]
            items.insert(LAST_KEYS, items.pop(LAST_KEYS + 1))
            counts = [0, 0, 2, 2, 2, 2] * (NCH - 1) + [2, 3, 3, 0, 0, 0]
            assert len(counts) == NPR and sum(counts) == NJB
            n = 0
            for index, ((what, c, i), count) in enumerate(zip(items, counts)):
                yield what, index, c, i, list(range(n, n + count))
                n += count

        def key_pieces(m):
            return ((m, slice(0, HD), slice(0, HD)), (KV - 1, slice(HD, P), slice(m * TAIL, (m + 1) * TAIL)))

        def column_parts(g):
            if g in (0, NG - 1):
                return (slice(0, BANK), False), (slice(BANK, GQ), True)
            return ((slice(0, GQ), True),)

        def halves(b, g):
            return 2 * b + (1 if g == 0 else 2)

        def projected(b, n):
            return 2 * (b * NPR + n)

        def h_parts(c):
            return (slice(0, NC // 2), slice(NC // 2, NC)) if c == 0 else (slice(0, NC),)

        def even(w):
            return w + w % 2

        H_PARTS_AHEAD = sum(len(h_parts(c)) for c in range(H_AHEAD))
        block = ctx.enter_context(nc.Block())

        @block.gpsimd
        def _(pool):
            pool.sem_inc(q_split, CREDIT)

            def load_q(b, kv):
                pool.wait_ge(q_split, CREDIT + b * KV + kv)
                pool.dma_start(q_raw[:], q_v[:, kv * G:(kv + 1) * G, bass.ds(b * Q, Q)]).then_inc(q_loaded, 16)

            def load_h(b, c):
                s0, w = CHUNKS[c]
                pool.wait_ge(h_split, CREDIT + b * (NCH + 1) + (c if c >= 2 else 0))
                wc = min(w, CTX - s0)
                pool.dma_start(h_raw[:, c % 2, :, 0:wc], ctx_v[:, bass.ds(b * NC, NC), s0:s0 + wc]).then_inc(h_loaded[c % 2], 16)
                if wc < w:
                    pool.dma_start(h_raw[:, c % 2, :, wc:w], xt_v[:, :, bass.ds(b * Q, Q)]).then_inc(h_loaded[c % 2], 16)

            def split_q(b, kv):
                pool.wait_ge(q_hi_done, b * KV + kv + 1)
                nc.gpsimd.tensor_tensor(q_lo[:, kv % 2, :], q_raw[:].rearrange("d g q -> d (g q)"),
                                        q_hi[0:HD, kv % 2, :], ALU.subtract).then_inc(q_split, 1)

            def norm(b, kv):
                pool.wait_ge(l_spread, (b * KV + kv + 1) * 16)
                nc.gpsimd.tensor_tensor(o_sb[0:HD, :], o_sb[0:HD, :], l_bc[:], ALU.mult).then_inc(o_normed, 1)

            def batch(b, before):
                if before is not None:
                    load_h(b, 0)
                if before is not None:
                    load_q(b, 0)
                    load_h(b, 1)
                    split_q(b, 0)
                    load_q(b, 1)
                load_h(b, 2)
                load_h(b, 3)
                if before is not None:
                    norm(before, KV - 1)
                else:
                    nc.gpsimd.memset(v_hi[:, :, :, HD:R].bitcast(F32), 1.0).then_inc(ones_set, 1)
                    pool.wait_ge(ones_set, 1)
                    nc.gpsimd.memset(v_lo[:, :, :, HD:R].bitcast(F32), 0.0).then_inc(ones_set, 1)
                    pool.wait_ge(ones_set, 2)
                    nc.gpsimd.memset(kt_hi[HD:R, :, :].bitcast(F32), 1.0).then_inc(ones_set, 1)
                    for stored in q_stored:
                        pool.wait_ge(stored, 16 * (KV * QS // P) * (B * Q // BANK) // len(q_stored))
                    split_q(b, 0)
                    load_q(b, 1)
                load_h(b, 4)
                for kv in range(KV):
                    if kv + 1 < KV:
                        split_q(b, kv + 1)
                    if kv + 2 < KV:
                        load_q(b, kv + 2)
                    if kv > 0:
                        norm(b, kv - 1)

            batch(0, None)
            with pool.Fori(0, B - 1) as b:
                batch(b + 1, b)

        @block.sync
        def _(sp):
            sp.sem_inc(o_sb_free, CREDIT)
            def place_m(b, kv):
                sp.wait_ge(m_row_done, b * KV + kv + 1)
                sp.dma_start(q_hi[HD:R, kv % 2, :].bitcast(F32).rearrange("o (j t) -> o j t", j=NJ),
                             m_row[:].bitcast(F32)).then_inc(m_row_placed, 16)

            def spread_sums(b, kv):
                n = b * KV + kv + 1
                sp.wait_ge(o_copied, CREDIT + 2 * n)
                sp.dma_start(l_rows[:], o_sb[HD:R, :].rearrange("o (j t) -> o j t", j=32)).then_inc(l_moved, 16)
                sp.wait_ge(l_inverted, n)
                sp.dma_start(l_dram.rearrange("(j t) -> j t", j=32), l_inv[:]).then_inc(l_stored, 16)
                sp.wait_ge(l_stored, n * 16)
                sp.dma_start(l_bc[:], l_dram.partition_broadcast(HD)).then_inc(l_spread, 16)
                sp.wait_ge(o_normed, n)
                sp.dma_start(o_v[:, kv * G:(kv + 1) * G, bass.ds(b * Q, Q)],
                             o_sb[0:HD, :].rearrange("d (g q) -> d g q", g=G)).then_inc(o_stored, 16)
                sp.wait_ge(o_stored, n * 16)
                sp.sem_inc(o_sb_free, 1)

            with sp.Fori(0, B - 1) as b:
                place_m(b, 0)
                place_m(b, 1)
                for kv in range(KV):
                    spread_sums(b, kv)
                    if kv + 2 < KV:
                        place_m(b, kv + 2)
            b = B - 1
            place_m(b, 0)
            sp.wait_ge(h_split, CREDIT + B * (NCH + 1))
            for part in range(WO_AHEAD):
                sp.dma_start(landed(h_raw, part, KP, D), wo_v[:, part * KP:(part + 1) * KP, :]).then_inc(wo_loaded, 16)
            place_m(b, 1)
            for kv in range(KV - 1):
                if kv == KV - 2:
                    sp.wait_ge(pv_done, CREDIT + b * NG + (KV - 1) * NTL)
                    for n in range(O_AHEAD):
                        sp.dma_start(attended_tile(v_lo, n, NK).bitcast(F32), o_tiles[:, :, n * P:(n + 1) * P]).then_inc(tile_loaded, 16)
                spread_sums(b, kv)
                if kv + 2 < KV:
                    place_m(b, kv + 2)
            sp.wait_ge(piece_split, WO_PIECES)
            for n in range(2):
                part = WO_AHEAD + n
                sp.dma_start(landed(h_raw, n, KP, D), wo_v[:, part * KP:(part + 1) * KP, :]).then_inc(wo_rest_loaded, 16)
            sp.wait_ge(wo_rest_loaded, 32)

        @block.scalar
        def _(act):
            def split_q(b, kv, loaded=False):
                if not loaded:
                    act.wait_ge(q_loaded, (b * KV + kv) * 16)
                nc.scalar.activation(q_hi[0:HD, kv % 2, :], q_raw[:].rearrange("d g q -> d (g q)"),
                                     ACT.Copy).then_inc(q_hi_done, 1)

            def split_h(b, c):
                if c >= 2:
                    act.wait_ge(pr_done, b * NPR + PC * (c - 1))
                per = (64, 32)[c % 2]
                act.wait_ge(h_loaded[c % 2], b * per + (16 * (c // 2 + 1) if c < NCH - 1 else per) - 16)
                w = even(CHUNKS[c][1])
                for n, part in enumerate(h_parts(c)):
                    if c < 2:
                        act.wait_ge(pv_done, CREDIT + b * NG - (2 - n if c == 0 else 0))
                    nc.scalar.activation(h_at(0, c)[:, part, 0:w], h_raw[:, c % 2, part, 0:w], ACT.Copy).then_inc(h_hi_done, 1)

            def project(b, before):
                if before is not None:
                    for c in range(H_AHEAD):
                        split_h(b, c)
                split_q(b, 0, loaded=before is None)
                if before is None:
                    act.wait_ge(table_set, 1)
                    nc.scalar.activation(table[:], table[:], ACT.Exp)
                for what, n, c, i, _jobs in projections():
                    s0, w = CHUNKS[c]
                    w = even(w)
                    if n == NPR - 2:
                        split_q(b, 1)
                    if n == NPR - 1:
                        exps(b, 0)
                    act.wait_ge(pr_done, b * NPR + n + 1)
                    if what == "k":
                        for kv, src, dst in key_pieces(i):
                            nc.scalar.activation(kt_hi[dst, kv, s0:s0 + w], pr_ps[n % NB][src, 0:w], ACT.Copy).then_inc(pr_hi_done, 1)
                    else:
                        m = TILES[i][1]
                        nc.scalar.activation(v_hi[0:m, i, :, 0:HD], pr_ps[n % NB][0:m, 0:KVD].rearrange("p (k d) -> p k d", k=KV),
                                             ACT.Copy).then_inc(pr_hi_done, 2)
                    if n % PC == 1 and 0 < c < NCH - 1:
                        split_h(b, c + 1)

            def exps(b, g):
                m = TILES[g % NTL][1]
                act.wait_ge(s_done, b * NG + g + 1)
                if g >= PSLOTS:
                    act.wait_ge(pv_done, CREDIT + b * NG + g - PSLOTS + 1)
                if g == 1:
                    act.wait_ge(pr_done, (b + 1) * NPR)
                s_in = s_ps[0:m, g % 2, :, :].rearrange("p a n -> p (a n)")
                for cols, whole in column_parts(g):
                    nc.scalar.activation(p_at(0, g)[0:m, cols], s_in[:, cols], ACT.Exp, scale=SCALE)
                    nc.scalar.activation(s_in[:, cols], s_in[:, cols], ACT.Exp, scale=SCALE).then_inc(
                        exp_done if whole else exp_half_done, 1)

            def attend(b, last=False):
                for g in range(NG):
                    kv, t = divmod(g, NTL)
                    if t == 2 and kv > 0:
                        act.wait_ge(pv_done, CREDIT + b * NG + kv * NTL)
                        act.wait_ge(o_sb_free, CREDIT + b * KV + kv - 1)
                        nc.scalar.activation(o_sb[:, BANK:], o_ps[0:R, 1, :], ACT.Copy).then_inc(o_copied, 1)
                    if g > 0:
                        exps(b, g)
                    if t == 0 and 0 < kv < KV - 1:
                        split_q(b, kv + 1)
                    if last and g // NTL == KV - 1 and piece(g % NTL) is not None:
                        kind, raw, hi, _lo = piece(g % NTL)
                        if kind == "weights":
                            act.wait_ge(wo_loaded, 16 * WO_AHEAD)
                        else:
                            act.wait_ge(tile_loaded, 16 * O_AHEAD)
                        nc.scalar.activation(hi, raw, ACT.Copy).then_inc(piece_hi_done, 1)

            act.sem_inc(h_hi_done, H_PARTS_AHEAD)
            project(0, None)
            with act.Fori(0, B - 1) as b:
                attend(b)
                project(b + 1, b)
            attend(B - 1, last=True)

        @block.vector
        def _(dve):
            dve.sem_inc(o_copied, CREDIT)
            dve.sem_inc(h_split, CREDIT + H_PARTS_AHEAD)
            nc.vector.memset(table[:], 0.0).then_inc(table_set, 1)
            dve.sem_inc(mm_reduced, CREDIT)

            def split_h(b, c):
                w = even(CHUNKS[c][1])
                for n, part in enumerate(h_parts(c)):
                    dve.wait_ge(h_hi_done, b * (NCH + 1) + (1 + n if c == 0 else c + 2))
                    nc.vector.tensor_tensor(h_at(1, c)[:, part, 0:w], h_raw[:, c % 2, part, 0:w], h_at(0, c)[:, part, 0:w],
                                            ALU.subtract).then_inc(h_split, 1)

            def reduce_job(b, kv, n):
                c, j = divmod(n, NJ)
                dve.wait_ge(mm_done, b * KV * NJB + kv * NJB + n + 1)
                nc.vector.reduce_max(m_part[:, j, c:c + 1], m_ps[:, n % 2, 0:CHUNKS[c][1]], AX_X).then_inc(mm_reduced, 1)

            def join_m(b, kv):
                dve.wait_ge(mm_reduced, CREDIT + b * KV * NJB + (kv + 1) * NJB)
                nc.vector.reduce_max(m_all[:], m_part[:], AX_X).then_inc(m_all_done, 1)

            def finish_m(b, kv):
                dve.wait_ge(m_turned, b * KV + kv + 1)
                nc.vector.tensor_scalar(m_row[:], m_ps[0:NJ, 0, 0:P], -1.0, None, ALU.mult).then_inc(m_row_done, 1)

            def split_p(b, g):
                m = TILES[g % NTL][1]
                full = s_ps[0:m, g % 2, :, :].rearrange("p a n -> p (a n)")
                for cols, whole in column_parts(g):
                    if whole:
                        dve.wait_ge(exp_done, b * NG + g + 1)
                    else:
                        dve.wait_ge(exp_half_done, halves(b, g))
                    nc.vector.tensor_tensor(p_at(1, g)[0:m, cols], full[:, cols], p_at(0, g)[0:m, cols],
                                            ALU.subtract).then_inc(p_split if whole else p_half_split, 1)

            def invert_sums(b, kv):
                dve.wait_ge(l_moved, (b * KV + kv + 1) * 16)
                nc.vector.reciprocal(l_inv[:], l_rows[:]).then_inc(l_inverted, 1)

            def copy_o(b, kv):
                dve.wait_ge(pv_done, CREDIT + b * NG + (kv + 1) * NTL)
                dve.wait_ge(o_sb_free, CREDIT + b * KV + kv)
                if kv < KV - 1:
                    nc.vector.tensor_copy(o_sb[:, 0:BANK], o_ps[0:R, 0, :]).then_inc(o_copied, 1)
                else:
                    nc.vector.tensor_copy(o_sb[:], o_ps[0:R, :, :].rearrange("p a n -> p (a n)")).then_inc(o_copied, 2)

            def split_projection(b, what, n, i, s0, w):
                if what == "k":
                    for k, (kv, src, dst) in enumerate(key_pieces(i)):
                        dve.wait_ge(pr_hi_done, projected(b, n) + 1 + k)
                        nc.vector.tensor_tensor(kt_lo[dst, kv, s0:s0 + w], pr_ps[n % NB][src, 0:w],
                                                kt_hi[dst, kv, s0:s0 + w], ALU.subtract).then_inc(pr_split, 1)
                else:
                    m = TILES[i][1]
                    dve.wait_ge(pr_hi_done, projected(b, n + 1))
                    nc.vector.tensor_tensor(v_lo[0:m, i, :, 0:HD], pr_ps[n % NB][0:m, 0:KVD].rearrange("p (k d) -> p k d", k=KV),
                                            v_hi[0:m, i, :, 0:HD], ALU.subtract).then_inc(pr_split, 2)

            def project(b, before):
                if before is not None:
                    for c in range(H_AHEAD):
                        split_h(b, c)
                due = None
                for what, n, c, i, jobs in projections():
                    s0, w = CHUNKS[c]
                    w = even(w)
                    early = 0 if n == LAST_KEYS + 1 else 2
                    for job in jobs[:early]:
                        reduce_job(b, 0, job)
                    if due is not None:
                        split_projection(b, *due)
                    due = (what, n, i, s0, w)
                    for job in jobs[early:]:
                        reduce_job(b, 0, job)
                    if n % PC == 2 and 0 < c < NCH - 1:
                        split_h(b, c + 1)
                    if n == NPR - 4:
                        join_m(b, 0)
                    if n == NPR - 3:
                        finish_m(b, 0)
                    if before is not None and n == 2:
                        copy_o(before, KV - 1)
                    if before is not None and n == PC:
                        invert_sums(before, KV - 1)
                split_p(b, 0)
                split_projection(b, *due)

            def attend(b, last=False):
                for g in range(NG + 1):
                    kv, t = divmod(g, NTL)
                    if t == 2 and 0 < kv < KV:
                        copy_o(b, kv - 1)
                    if g >= 2:
                        split_p(b, g - 1)
                    of_t = (g - 1) % NTL
                    if last and g > (KV - 1) * NTL and piece(of_t) is not None:
                        _kind, raw, hi, lo = piece(of_t)
                        dve.wait_ge(piece_hi_done, of_t - PIECES_AT + 1)
                        nc.vector.tensor_tensor(lo, raw, hi, ALU.subtract).then_inc(piece_split, 1)
                    if t == INVERT_AT and kv > 0:
                        invert_sums(b, kv - 1)
                    for job in jobs_of(g):
                        reduce_job(b, *job)
                    if t == M_AT and kv + 1 < KV:
                        join_m(b, kv + 1)
                        finish_m(b, kv + 1)

            project(0, None)
            with dve.Fori(0, B - 1) as b:
                attend(b)
                project(b + 1, b)
            attend(B - 1, last=True)

        @block.tensor
        def _(pe):
            pe.sem_inc(pv_done, CREDIT)

            def job(b, kv, n):
                c, j = divmod(n, NJ)
                s0, w = CHUNKS[c]
                w = even(w)
                if kv > 0 or n >= 2:
                    pe.wait_ge(mm_reduced, CREDIT + b * KV * NJB + kv * NJB + n - 1)
                nc.tensor.matmul(m_ps[:, n % 2, 0:w], q_hi[0:HD, kv % 2, j * P:(j + 1) * P], kt_hi[0:HD, kv, s0:s0 + w],
                                 start=True, stop=True).then_inc(mm_done, 1)

            def nothing():
                pass

            def first_job(b, n):
                if n % NJ == 0:
                    pe.wait_ge(q_hi_done, b * KV + 1)
                    c = n // NJ
                    pe.wait_ge(pr_split, projected(b, c * PC if c < NCH - 1 else LAST_KEYS) + 1)
                job(b, 0, n)

            def turn_m(b, kv):
                pe.wait_ge(m_all_done, b * KV + kv + 1)
                nc.tensor.transpose(m_ps[0:NJ, 0, 0:P], m_all[:], ident[:]).then_inc(m_turned, 1)

            def scores(g, half):
                kv, t = divmod(g, NTL)
                s0, m = TILES[t]
                keys = slice(s0, s0 + m)
                cols = slice(half * BANK, (half + 1) * BANK)
                out = s_ps[0:m, g % 2, half, :]
                nc.tensor.matmul(out, kt_hi[0:R, kv, keys], q_hi[0:R, kv % 2, cols], start=True, stop=False)
                nc.tensor.matmul(out, kt_hi[0:HD, kv, keys], q_lo[0:HD, kv % 2, cols], start=False, stop=False)
                return nc.tensor.matmul(out, kt_lo[0:HD, kv, keys], q_hi[0:HD, kv % 2, cols], start=False, stop=True)

            def values(g, half):
                kv, t = divmod(g, NTL)
                m = TILES[t][1]
                cols = slice(half * BANK, (half + 1) * BANK)
                pairs = three_passes(v_hi[0:m, t, kv, :], v_lo[0:m, t, kv, :], p_at(0, g)[0:m, cols], p_at(1, g)[0:m, cols])
                for n, (stationary, moving) in enumerate(pairs):
                    last = nc.tensor.matmul(o_ps[0:R, half, :], stationary, moving,
                                            start=(t == 0 and n == 0), stop=(t == NTL - 1 and n == 2))
                return last

            def first_scores(b):
                pe.wait_ge(ones_set, 3)
                pe.wait_ge(m_row_placed, (b * KV + 1) * 16)
                pe.wait_ge(q_split, CREDIT + b * KV + 1)
                pe.wait_ge(pr_split, projected(b, NPR - 3))
                scores(0, 0)
                scores(0, 1).then_inc(s_done, 1)

            def project(b):
                for what, n, c, i, jobs in projections():
                    s0, w = CHUNKS[c]
                    w = even(w)
                    if what == "k" and i == 0 and c > 0:
                        pe.wait_ge(h_split, CREDIT + b * (NCH + 1) + c + 2)
                    h_hi, h_lo = h_at(0, c), h_at(1, c)
                    if n >= NB:
                        pe.wait_ge(pr_split, projected(b, n - NB + 1))
                    elif n >= 4:
                        pe.wait_ge(o_copied, CREDIT + b * KV * 2)
                    between = [lambda job=job: first_job(b, job) for job in jobs]
                    if n == LAST_KEYS + 1:
                        between = [nothing] * 4 + between
                    elif jobs:
                        between = [between[0], between[1], nothing, *between[2:]]
                    if n == NPR - 3:
                        between = [lambda: turn_m(b, 0), nothing, nothing]
                    if n == NPR - 1:
                        first_scores(b)
                    if what == "k":
                        rows = slice(i * P, (i + 1) * P)
                        if n == 0:
                            pe.wait_ge(h_split, CREDIT + b * (NCH + 1) + 1)
                            between = [lambda: pe.wait_ge(h_split, CREDIT + b * (NCH + 1) + 2)]
                        last = split_product(nc, pr_ps[n % NB][:, 0:w],
                                             [(wk_hi[:, k, rows], wk_lo[:, k, rows], h_hi[:, k, 0:w], h_lo[:, k, 0:w])
                                              for k in range(NC)], between)
                    else:
                        m = TILES[i][1]
                        at = i % (CW // P) * P
                        last = split_product(nc, pr_ps[n % NB][0:m, 0:KVD],
                                             [(h_hi[:, k, at:at + m], h_lo[:, k, at:at + m], wv_hi[:, k, :], wv_lo[:, k, :])
                                              for k in range(NC)], between)
                    last.then_inc(pr_done, 1)

            def attend(b):
                for g in range(NG + 2):
                    kv, t = divmod(g, NTL)
                    jobs = jobs_of(g)
                    if jobs and t == JOBS_AT:
                        pe.wait_ge(q_hi_done, b * KV + kv + 2)
                    if 0 < g < NG:
                        if t == 0:
                            pe.wait_ge(m_row_placed, (b * KV + kv + 1) * 16)
                            pe.wait_ge(q_split, CREDIT + b * KV + kv + 1)
                        if g == 2:
                            pe.wait_ge(p_half_split, halves(b, 0))
                        elif g > 2:
                            pe.wait_ge(p_split, b * NG + g - 1)
                        if g == 1:
                            pe.wait_ge(pr_split, projected(b, NPR - 2))
                        scores(g, 0)
                        if g == 2:
                            pe.wait_ge(p_split, b * NG + 1)
                        if jobs:
                            job(b, *jobs[0])
                        scores(g, 1).then_inc(s_done, 1)
                        if jobs:
                            job(b, *jobs[1])
                    if g >= 2:
                        if g == NG:
                            pe.wait_ge(p_split, b * NG + g - 1)
                        elif g > NG:
                            pe.wait_ge(p_half_split, halves(b, NG - 1))
                        if g == 2:
                            pe.wait_ge(pr_split, projected(b, NPR))
                        if (g - 2) % NTL == 0:
                            pe.wait_ge(o_copied, CREDIT + (b * KV + kv) * 2)
                        values(g - 2, 0)
                        if g > NG:
                            pe.wait_ge(p_split, (b + 1) * NG)
                        if t == M_AT and kv + 1 < KV:
                            turn_m(b, kv + 1)
                        if jobs:
                            job(b, *jobs[2])
                            job(b, *jobs[3])
                        values(g - 2, 1).then_inc(pv_done, 1)

            project(0)
            with pe.Fori(0, B - 1) as b:
                attend(b)
                project(b + 1)
            attend(B - 1)


def output_router_experts(nc, x, wg, bg, we, be, earlier_in, wkv, ident, landing, work, spare, values_sb, tail, banks, l_dram, o_dram,
                          out, QD, G, Q):
    T, D = x.shape
    E, _, H = we.shape
    NT, NC, NK = T // P, D // P, QD // P
    KP = NK // PARTS
    E0, T0 = 2 * NT, 2
    x_v = x.rearrange("(t p) d -> t p d", p=P)
    o_v = o_dram.rearrange("(k p) t -> p k t", p=P)
    we_v = we.rearrange("e (c p) h -> p (e c) h", p=P)
    out_v = out.rearrange("(t p) h -> t p h", p=P)
    assert E % 2 == 0 and H == D == BANK and NT == 8 and landing.shape[2] * landing.shape[3] * 2 >= NC * (H + 2 * P)

    with ExitStack() as ctx:
        def sb(name, shape, dt=F32):
            return ctx.enter_context(nc.sbuf_tensor(name, shape, dt))

        def sem(name):
            return ctx.enter_context(nc.semaphore(name))

        x1 = sb("x1", [P, NT, D])
        x2_hi = sb("x2_hi", [P, NC, T], F32R)
        x2_lo = sb("x2_lo", [P, NC, T], F32R)
        weight = sb("weight", [P, NT * E])
        wg_sb = sb("o_wg", [P, NC, E])
        bg_bc = sb("o_bg", [P, E])
        earlier = sb("o_earlier", [P, E, E])
        wo_rest_hi, wo_rest_lo = [work[:, part, 0:2 * KP * D].rearrange("p (n k d) -> p n k d", n=2, k=KP) for part in (0, 1)]
        wo_at = output_weights(wkv, KP, D) + [(wo_rest_hi[:, n, :, :], wo_rest_lo[:, n, :, :]) for n in range(2)]
        v_hi, v_lo = values_sb
        SLOTS = 3
        o_hi = [attended_tile(v_hi, n, NK) for n in range(SLOTS)]
        o_lo = [attended_tile(v_lo, n, NK) for n in range(SLOTS)]
        o_sb, l_rows, l_inv, l_bc = tail
        HD = l_bc.shape[0]
        x_sb = sb("o_x", [P, 2, D])
        stats = sb("o_stats", [P, NT, 6])
        mean_var = sb("o_mean_var", [P, NT, 2])
        var_eps = sb("o_var_eps", [P, NT])
        std = sb("o_std", [P, NT])
        rstd = sb("o_rstd", [P, NT])
        xn = sb("o_xn", [P, 2, D])
        logits = sb("o_logits", [P, 2, E])
        above = sb("o_above", [P, E, E])
        same = sb("o_same", [P, E, E])
        rank = sb("o_rank", [P, E])
        def flat(v, at):
            return v[:].rearrange("p t k r -> p (t k r)")[:, at:at + NC * H].rearrange("p (c h) -> p c h", c=NC)

        we_hi_even = sb("e_w_hi", [P, NC, H], F32R)
        we_lo_even = sb("e_w_lo", [P, NC, H], F32R)
        landing_flat = landing[:].rearrange("p s c m -> p (s c m)")
        we_raw = landing_flat[:, 0:NC * H].rearrange("p (c h) -> p c h", c=NC)
        x2_raw = landing_flat[:, NC * H:NC * H + 2 * NC * P].rearrange("p (s c t) -> p s c t", s=2, c=NC)
        we_hi = [we_hi_even[:], flat(v_hi, 0)]
        we_lo = [we_lo_even[:], flat(v_hi, NC * H)]
        b_bc = spare[:, 0:2, :]
        z, r = x_sb, xn
        y_at = [banks[:, n, :] for n in (2, 3)]
        g_at = [banks[:, n, 0:E] for n in (4, 5)]
        x2_at = [banks[:, n, :].rearrange("p (c t) -> p c t", c=NC) for n in (6, 7)]

        o_copied = sem("t_o_copied")
        l_moved = sem("t_l_moved")
        l_inverted = sem("t_l_inverted")
        l_stored = sem("t_l_stored")
        l_spread = sem("t_l_spread")
        o_normed = sem("t_o_normed")
        o_stored = sem("t_o_stored")

        wg_loaded = sem("o_wg_loaded")
        const_loaded = sem("o_const_loaded")
        wo_hi_done = sem("o_w_hi_done")
        wo_split = sem("o_w_split")
        o_loaded = [sem(f"o_loaded{s}") for s in range(SLOTS)]
        x_loaded = [sem(f"o_x_loaded{s}") for s in range(2)]
        o_hi_done = sem("o_hi_done")
        o_split = sem("o_split")
        att_done = sem("o_att_done")
        x1_done = sem("o_x1_done")
        stats_done = sem("o_stats_done")
        mean_var_done = sem("o_mean_var_done")
        var_eps_done = sem("o_var_eps_done")
        std_done = sem("o_std_done")
        rstd_done = sem("o_rstd_done")
        xn_done = sem("o_xn_done")
        x2_turned = sem("o_x2_turned")
        x2_raw_done = sem("o_x2_raw_done")
        x2_split = sem("o_x2_split")
        g_done = sem("o_g_done")
        logits_done = sem("o_logits_done")
        rank_step = sem("o_rank_step")
        weight_done = sem("o_weight_done")
        we_loaded = sem("e_w_loaded")
        b_loaded = [sem(f"e_b_loaded{s}") for s in range(2)]
        we_hi_done = sem("e_w_hi_done")
        we_split = sem("e_w_split")
        y_done = sem("e_y_done")
        z_done = sem("e_z_done")
        r_done = sem("e_r_done")
        added = sem("e_added")
        stored = sem("e_stored")

        block = ctx.enter_context(nc.Block())
        steps = range(-3, NT + 1)
        AHEAD = 2
        EXPERT_AT = 3
        last_q = slice(x.shape[0] - Q, x.shape[0])
        last_heads = slice(QD // HD - G, QD // HD)

        @block.gpsimd
        def _(pool):
            pool.wait_ge(l_spread, 16)
            nc.gpsimd.tensor_tensor(o_sb[0:HD, :], o_sb[0:HD, :], l_bc[:], ALU.mult).then_inc(o_normed, 1)

        @block.sync
        def _(sp):
            def load_o(n):
                sp.dma_start(o_lo[n % SLOTS].bitcast(F32), o_v[:, :, n * P:(n + 1) * P]).then_inc(o_loaded[n % SLOTS], 16)

            def load_x(n):
                sp.dma_start(x_sb[:, n % 2, :], x_v[n]).then_inc(x_loaded[n % 2], 16)

            def load_we(e):
                sp.dma_start(we_raw, we_v[:, bass.ds(e * NC, NC), :]).then_inc(we_loaded, 16)

            def load_b(e, s):
                sp.dma_start(b_bc[:, s, :], be[bass.ds(e, 1), :].squeeze(0).partition_broadcast(P)).then_inc(b_loaded[s], 16)

            load_x(0)
            sp.wait_ge(o_copied, 1)
            sp.dma_start(l_rows[:], o_sb[HD:HD + 1, :].rearrange("o (j t) -> o j t", j=32)).then_inc(l_moved, 16)
            load_o(2)
            load_x(1)
            sp.dma_start(wg_sb[:], wg.rearrange("(c p) e -> p c e", p=P)).then_inc(wg_loaded, 16)
            sp.wait_ge(l_inverted, 1)
            sp.dma_start(l_dram.rearrange("(j t) -> j t", j=32), l_inv[:]).then_inc(l_stored, 16)
            sp.wait_ge(l_stored, 16)
            sp.dma_start(l_bc[:], l_dram.partition_broadcast(HD)).then_inc(l_spread, 16)
            sp.dma_start(bg_bc[:], bg.partition_broadcast(P)).then_inc(const_loaded, 16)
            sp.dma_start(earlier[:], earlier_in.rearrange("p (e j) -> p e j", e=E)).then_inc(const_loaded, 16)
            sp.wait_ge(o_normed, 1)
            sp.dma_start(o_dram.rearrange("(h d) t -> d h t", d=HD)[:, last_heads, last_q],
                         o_sb[0:HD, :].rearrange("d (g q) -> d g q", g=G)).then_inc(o_stored, 16)
            sp.wait_ge(wo_split, 2)
            load_we(0)
            load_b(0, 0)
            load_b(1, 1)
            sp.wait_ge(o_stored, 16)
            for n in range(2, NT):
                if n + 1 < NT:
                    sp.wait_ge(att_done, n - 1)
                    load_o(n + 1)
                sp.wait_ge(x1_done, n - 1)
                load_x(n)
            sp.wait_ge(we_split, T0 + 1)
            load_we(1)
            with sp.Fori(0, E // 2 - 1) as pair:
                for s in range(2):
                    e = pair * 2 + (2 + s)
                    sp.wait_ge(we_split, T0 + e)
                    load_we(e)
                    sp.wait_ge(z_done, E0 + (e - 1) * NT)
                    load_b(e, s)
            for t in range(NT):
                sp.wait_ge(added, T0 + (E - 1) * NT + t + 1)
                sp.dma_start(out_v[t], x1[:, t, :]).then_inc(stored, 16)
            sp.wait_ge(stored, 16 * NT)

        @block.scalar
        def _(act):
            act.sem_inc(r_done, T0)

            def round_wo(n):
                nc.scalar.activation(wo_rest_hi[:, n, :, :], landed(landing, n, KP, D), ACT.Copy).then_inc(wo_hi_done, 1)

            def round_we(e, s):
                act.wait_ge(we_loaded, (e + 1) * 16)
                act.wait_ge(y_done, E0 + (e - 1) * NT)
                nc.scalar.activation(we_hi[s], we_raw, ACT.Copy).then_inc(we_hi_done, 1)

            for n in range(2):
                round_wo(n)
            for n in steps:
                if 0 <= n < NT:
                    act.wait_ge(x2_turned, n + 1)
                    nc.scalar.activation(x2_hi[:, :, n * P:(n + 1) * P], x2_at[n % 2], ACT.Copy)
                    if n >= 2:
                        act.wait_ge(g_done, n - 1)
                    nc.scalar.activation(x2_raw[:, n % 2, :, :], x2_at[n % 2], ACT.Copy).then_inc(x2_raw_done, 1)
                if 0 <= n + 1 < NT:
                    act.wait_ge(var_eps_done, n + 2)
                    nc.scalar.activation(std[:, n + 1:n + 2], var_eps[:, n + 1:n + 2], ACT.Sqrt).then_inc(std_done, 1)
                i = n + 3
                if AHEAD <= i < NT:
                    act.wait_ge(o_loaded[i % SLOTS], 16 * (i // SLOTS + (1 if i % SLOTS >= AHEAD else 0)))
                    nc.scalar.activation(o_hi[i % SLOTS], o_lo[i % SLOTS].bitcast(F32), ACT.Copy).then_inc(o_hi_done, 1)
                if n == EXPERT_AT:
                    round_we(0, 0)
            act.wait_ge(att_done, NT)

            def pair_of(e0, more):
                for s in range(2):
                    for t in range(NT):
                        if t == 1 and (s == 0 or more):
                            round_we(e0 + s + 1, 1 - s)
                        n = (e0 + s) * NT + t
                        act.wait_ge(z_done, E0 + n + 1)
                        act.wait_ge(added, T0 + n - 1)
                        nc.scalar.activation(r[:, t % 2, :], z[:, t % 2, :], ACT.Relu,
                                             scale=weight[:, bass.ds(e0 + (t * E + s), 1)]).then_inc(r_done, 1)

            act.wait_ge(weight_done, NT)
            with act.Fori(0, E // 2 - 1) as pair:
                pair_of(pair * 2, True)
            pair_of(E - 2, False)

        @block.vector
        def _(dve):
            dve.sem_inc(z_done, E0)
            dve.sem_inc(added, T0)
            dve.sem_inc(we_split, T0)

            def split_wo(n):
                dve.wait_ge(wo_hi_done, n + 1)
                nc.vector.tensor_tensor(wo_rest_lo[:, n, :, :], landed(landing, n, KP, D), wo_rest_hi[:, n, :, :],
                                        ALU.subtract).then_inc(wo_split, 1)

            def split_we(e, s):
                dve.wait_ge(we_hi_done, e + 1)
                nc.vector.tensor_tensor(we_lo[s], we_raw, we_hi[s], ALU.subtract).then_inc(we_split, 1)

            def route(n):
                i = n % 2
                steps_before = 5 * n
                shape = [P, E, E]
                of_other = logits[:, i, :].rearrange("p (o j) -> p o j", o=1).to_broadcast(shape)
                of_this = logits[:, i, :].rearrange("p (e o) -> p e o", o=1).to_broadcast(shape)
                nc.vector.tensor_tensor(above[:], of_other, of_this, ALU.is_gt).then_inc(rank_step, 1)
                nc.vector.tensor_tensor(same[:], of_other, of_this, ALU.is_equal).then_inc(rank_step, 1)
                dve.wait_ge(rank_step, steps_before + 2)
                nc.vector.tensor_tensor(same[:], same[:], earlier[:], ALU.mult).then_inc(rank_step, 1)
                dve.wait_ge(rank_step, steps_before + 3)
                nc.vector.tensor_tensor(above[:], above[:], same[:], ALU.add).then_inc(rank_step, 1)
                dve.wait_ge(rank_step, steps_before + 4)
                nc.vector.reduce_sum(rank[:], above[:], AX_X).then_inc(rank_step, 1)
                dve.wait_ge(rank_step, steps_before + 5)
                nc.vector.tensor_scalar(weight[:, n * E:(n + 1) * E], rank[:], TOP_K - 0.5, 1.0 / TOP_K,
                                        ALU.is_lt, ALU.mult).then_inc(weight_done, 1)

            nc.vector.tensor_copy(o_sb[:], banks[0:HD + 1, 4:6, :].rearrange("p a n -> p (a n)")).then_inc(o_copied, 1)
            split_wo(0)
            dve.wait_ge(l_moved, 16)
            nc.vector.reciprocal(l_inv[:], l_rows[:]).then_inc(l_inverted, 1)
            split_wo(1)
            for n in steps:
                i = n + 1
                if 0 <= i < NT:
                    dve.wait_ge(att_done, i + 1)
                    dve.wait_ge(x_loaded[i % 2], 16 * (i // 2 + 1))
                    nc.vector.tensor_tensor(x1[:, i, :], y_at[i % 2], x_sb[:, i % 2, :], ALU.add).then_inc(x1_done, 1)
                    dve.wait_ge(x1_done, i + 1)
                    nc.vector.bn_stats(stats[:, i, :], x1[:, i, :]).then_inc(stats_done, 1)
                    dve.wait_ge(stats_done, i + 1)
                    nc.vector.bn_aggr(mean_var[:, i, :], stats[:, i, :]).then_inc(mean_var_done, 1)
                    dve.wait_ge(mean_var_done, i + 1)
                    nc.vector.tensor_scalar_add(var_eps[:, i:i + 1], mean_var[:, i, 1:2], EPS).then_inc(var_eps_done, 1)
                if 0 <= n < NT:
                    dve.wait_ge(x2_raw_done, n + 1)
                    tok = slice(n * P, (n + 1) * P)
                    nc.vector.tensor_tensor(x2_lo[:, :, tok], x2_at[n % 2], x2_hi[:, :, tok], ALU.subtract).then_inc(x2_split, 1)
                if 0 <= i < NT:
                    dve.wait_ge(std_done, i + 1)
                    nc.vector.reciprocal(rstd[:, i:i + 1], std[:, i:i + 1]).then_inc(rstd_done, 1)
                    dve.wait_ge(rstd_done, i + 1)
                    if i >= 2:
                        dve.wait_ge(x2_turned, i - 1)
                    nc.vector.tensor_scalar(xn[:, i % 2, :], x1[:, i, :], mean_var[:, i, 0:1], rstd[:, i:i + 1],
                                            ALU.subtract, ALU.mult).then_inc(xn_done, 1)
                if n >= 1:
                    if n == 1:
                        dve.wait_ge(const_loaded, 32)
                    dve.wait_ge(g_done, n)
                    nc.vector.tensor_tensor(logits[:, (n - 1) % 2, :], g_at[(n - 1) % 2], bg_bc[:], ALU.add).then_inc(logits_done, 1)
                    dve.wait_ge(logits_done, n)
                    route(n - 1)
                k = n + 3
                if AHEAD <= k < NT:
                    dve.wait_ge(o_hi_done, k - AHEAD + 1)
                    nc.vector.tensor_tensor(o_lo[k % SLOTS], o_lo[k % SLOTS].bitcast(F32), o_hi[k % SLOTS],
                                            ALU.subtract).then_inc(o_split, 1)
                if n == EXPERT_AT:
                    split_we(0, 0)

            def add_bias(n, s, t):
                dve.wait_ge(y_done, E0 + n + 1)
                dve.wait_ge(r_done, T0 + n - 1)
                nc.vector.tensor_tensor(z[:, t % 2, :], banks[:, t, :], b_bc[:, s, :], ALU.add).then_inc(z_done, 1)

            def accumulate(n, t):
                dve.wait_ge(r_done, T0 + n + 1)
                nc.vector.tensor_tensor(x1[:, t, :], x1[:, t, :], r[:, t % 2, :], ALU.add).then_inc(added, 1)

            def pair_of(e0, more):
                for s in range(2):
                    e = e0 + s
                    dve.wait_ge(b_loaded[s], e0 * 8 + 16)
                    for t in range(NT):
                        add_bias(e * NT + t, s, t)
                        if t > 0:
                            accumulate(e * NT + t - 1, t - 1)
                        if t == 1 and (s == 0 or more):
                            split_we(e + 1, 1 - s)
                    accumulate(e * NT + NT - 1, NT - 1)

            with dve.Fori(0, E // 2 - 1) as pair:
                pair_of(pair * 2, True)
            pair_of(E - 2, False)

        @block.tensor
        def _(pe):
            pe.sem_inc(y_done, E0)

            def route(n):
                pe.wait_ge(x2_raw_done, n + 1)
                if n == 0:
                    pe.wait_ge(wg_loaded, 16)
                if n >= 2:
                    pe.wait_ge(logits_done, n - 1)
                for c in range(NC):
                    last = nc.tensor.matmul(g_at[n % 2], x2_raw[:, n % 2, c, :], wg_sb[:, c, :], start=(c == 0), stop=(c == NC - 1))
                last.then_inc(g_done, 1)

            def expert_tile(e, s, t):
                tok = slice(t * P, (t + 1) * P)
                pe.wait_ge(z_done, E0 + (e - 1) * NT + t + 1)
                split_product(nc, banks[:, t, :], [(x2_hi[:, c, tok], x2_lo[:, c, tok], we_hi[s][:, c, :], we_lo[s][:, c, :])
                                                   for c in range(NC)]).then_inc(y_done, 1)

            def expert(e, s):
                pe.wait_ge(we_split, T0 + e + 1)
                for t in range(NT):
                    expert_tile(e, s, t)

            for n in steps:
                if 0 <= n < NT:
                    if n == NT - 1:
                        pe.wait_ge(we_split, T0 + 1)
                        expert_tile(0, 0, 0)
                    pe.wait_ge(xn_done, n + 1)
                    if n >= 2:
                        pe.wait_ge(x2_split, n - 1)
                    for c in range(NC):
                        last = nc.tensor.transpose(x2_at[n % 2][:, c, :], xn[:, n % 2, c * P:(c + 1) * P], ident[:])
                    last.then_inc(x2_turned, 1)
                if n >= 1:
                    if n == NT:
                        expert_tile(0, 0, 1)
                    route(n - 1)
                i = n + 2
                if 0 <= i < NT:
                    if i >= AHEAD:
                        pe.wait_ge(o_split, i - AHEAD + 1)
                        pe.wait_ge(x1_done, i - 1)
                    for k in range(NK):
                        part, row = divmod(k, KP)
                        w_hi, w_lo = wo_at[part]
                        if i == 0 and part >= 2 and row == 0:
                            pe.wait_ge(wo_split, part - 1)
                        for m, (stationary, moving) in enumerate(three_passes(
                                o_hi[i % SLOTS][:, k, :], o_lo[i % SLOTS][:, k, :], w_hi[:, row, :], w_lo[:, row, :])):
                            last = nc.tensor.matmul(y_at[i % 2], stationary, moving,
                                                    start=(k == 0 and m == 0), stop=(k == NK - 1 and m == 2))
                    last.then_inc(att_done, 1)

            for t in range(2, NT):
                if t == 4:
                    pe.wait_ge(logits_done, NT)
                if t == 6:
                    pe.wait_ge(x2_split, NT)
                expert_tile(0, 0, t)
            expert(1, 1)
            with pe.Fori(0, E // 2 - 1) as pair:
                for s in range(2):
                    expert(pair * 2 + (2 + s), s)


H_AHEAD = 2
PSLOTS = 4
PARTS = 4
TOP_K = 2
HEADS, GROUPS, HEAD_DIM = 16, 4, 96


def cross_attention_and_experts(nc, x, ctx_t, wq, wk, wv, wo, wg, bg, we, be, ident, earlier, out, queries):
    T, D = x.shape
    B = ctx_t.shape[0]
    G = HEADS // GROUPS
    NC, KVD = D // P, GROUPS * HEAD_DIM
    xt_dram = nc.dram_tensor("normed_latents_t", (D, T), F32).ap()
    q_dram = nc.dram_tensor("queries_t", (HEADS * HEAD_DIM, T), F32).ap()
    l_dram = nc.dram_tensor("softmax_sums", (G * queries,), F32).ap()
    o_dram = nc.dram_tensor("attended_t", (HEADS * HEAD_DIM, T), F32).ap()
    HD = HEAD_DIM
    tiles = -(-(ctx_t.shape[2] + queries) // P)
    with (
        nc.sbuf_tensor("identity_sb", [P, P], F32) as ident_sb,
        nc.sbuf_tensor("wk_hi", [P, NC, KVD], F32R) as wk_hi,
        nc.sbuf_tensor("wk_lo", [P, NC, KVD], F32R) as wk_lo,
        nc.sbuf_tensor("wv_hi", [P, NC, KVD], F32R) as wv_hi,
        nc.sbuf_tensor("wv_lo", [P, NC, KVD], F32R) as wv_lo,
        nc.sbuf_tensor("landing", [P, 2, NC, KVD], F32) as landing,
        nc.sbuf_tensor("work", [P, 2, PSLOTS * G * queries], F32R) as work,
        nc.sbuf_tensor("queries_landing", [HD, G, queries], F32) as q_raw,
        nc.sbuf_tensor("queries_leaving", [P, 3, BANK], F32) as q_sb,
        nc.semaphore("q_stored0") as q_stored0,
        nc.semaphore("q_stored1") as q_stored1,
        nc.semaphore("q_stored2") as q_stored2,
    ):
        q_stored = (q_stored0, q_stored1, q_stored2)
        wkv = (wk_hi, wk_lo, wv_hi, wv_lo)
        latent_norm_and_queries(nc, x, ctx_t, wq, wk, wv, ident, xt_dram, q_dram, wkv, ident_sb, landing, work,
                                q_raw, q_sb, q_stored, G * queries)
        with (
            nc.sbuf_tensor("values_hi", [P, tiles, GROUPS, HD + 1], F32R) as v_hi,
            nc.sbuf_tensor("values_lo", [P, tiles, GROUPS, HD + 1], F32R) as v_lo,
            nc.sbuf_tensor("group_result", [HD + 1, G * queries], F32) as o_sb,
            nc.sbuf_tensor("sums_rows", [32, G * queries // 32], F32) as l_rows,
            nc.sbuf_tensor("sums_inverse", [32, G * queries // 32], F32) as l_inv,
            nc.sbuf_tensor("sums_spread", [HD, G * queries], F32) as l_bc,
            nc.psum_tensor("banks", [P, 8, BANK], F32) as banks,
        ):
            values_sb, tail = (v_hi, v_lo), (o_sb, l_rows, l_inv, l_bc)
            attention(nc, ctx_t, wo, wkv, ident_sb, landing, work, q_raw, q_stored, values_sb, tail, banks, xt_dram,
                      q_dram, l_dram, o_dram, B, GROUPS, HD, G, queries)
            output_router_experts(nc, x, wg, bg, we, be, earlier, wkv, ident_sb, landing, work, q_sb, values_sb, tail, banks,
                                  l_dram, o_dram, out, HEADS * HD, G, queries)


def kernel(x, ctx_4096, L0_xattn_Wq, L0_xattn_Wk, L0_xattn_Wv, L0_xattn_Wo, L0_ffn_W_gate, L0_ffn_b_gate,
           L0_ffn_W_e, L0_ffn_b_e):
    import numpy as np
    import concourse.bacc as bacc
    from concourse.bass_utils import run_bass_kernel_spmd

    B, Q, D = x.shape
    E = L0_ffn_W_gate.shape[1]
    arrays = {
        "x": np.reshape(x, (B * Q, D)),
        "context_t": np.transpose(ctx_4096, (0, 2, 1)),
        "wq_t": np.transpose(L0_xattn_Wq),
        "wk_t": np.transpose(L0_xattn_Wk),
        "wv_t": np.transpose(L0_xattn_Wv),
        "wo_t": np.transpose(L0_xattn_Wo),
        "w_gate": L0_ffn_W_gate,
        "b_gate": L0_ffn_b_gate,
        "w_e": L0_ffn_W_e,
        "b_e": L0_ffn_b_e,
        "identity": np.eye(P, dtype=np.float32),
        "earlier": np.broadcast_to(np.tril(np.ones((E, E), np.float32), -1).reshape(1, E * E), (P, E * E)),
    }
    arrays = {name: np.ascontiguousarray(a) for name, a in arrays.items()}
    nc = bacc.Bacc("TRN2", target_bir_lowering=False, num_devices=1)
    args = [nc.dram_tensor(name, a.shape, mybir.dt.from_np(a.dtype), kind="ExternalInput").ap()
            for name, a in arrays.items()]
    out = nc.dram_tensor("out", (B * Q, D), F32, kind="ExternalOutput").ap()
    cross_attention_and_experts(nc, *args, out, Q)
    result = run_bass_kernel_spmd(nc, [arrays], core_ids=[0])
    return np.reshape(result.results[0]["out"], (B, Q, D))
```
